# Optimizing a Trainium2 kernel written in Bass

```python
import numpy as np
import jax
import jax.numpy as jnp

def _softmax(x, axis=-1):
    return jax.nn.softmax(x, axis=axis)

def _gelu(x):
    return jax.nn.gelu(x, approximate=True)

def _silu(x):
    return jax.nn.silu(x)

def _sigmoid(x):
    return jax.nn.sigmoid(x)

def _layernorm(x, axis=-1, eps=1e-05):
    m = jnp.mean(x, axis=axis, keepdims=True)
    v = jnp.var(x, axis=axis, keepdims=True)
    return (x - m) / jnp.sqrt(v + eps)

def _scatter_add(tgt, idx, src, axis=0):
    return tgt.at[idx].add(src)

def _segment_sum(src, seg, n):
    return jax.ops.segment_sum(src, seg, n)
kernel_name = 'mk_gnn_ffn_d1_gnn_r8_481e9d'

def setup_inputs(seed: int=0):
    np.random.seed(seed)
    _w = jnp.asarray

    def _rec_inputs():
        import jax
        import jax.numpy as jnp
        _gk = jax.random.key(seed)
        x = -0.0002117 + 1 * jax.random.normal(jax.random.fold_in(_gk, 1), (12500, 256), jnp.float32)
        src = jax.random.randint(jax.random.fold_in(_gk, 2), (200000,), 0, 12500, jnp.int32)
        dst = jnp.minimum((12500 * jax.random.uniform(jax.random.fold_in(_gk, 3), (200000,)) ** 2.0).astype(jnp.int32), 99999)
        _o = jnp.argsort(dst, stable=True)
        src = src[_o]
        dst = dst[_o]
        edge_weight = jax.random.uniform(jax.random.fold_in(_gk, 12), (200000,), jnp.float32, 0.0, 1)
        return (x, src, dst, edge_weight)
    x, src, dst, edge_weight = _rec_inputs()

    def _L0_gnn_setup():
        import jax, jax.numpy as jnp
        import numpy as np
        N_NODES = 12500
        N_EDGES = 400000
        NFEAT = 256
        NHID = 256

        def _gcn_layer(x, W, b, edge_weight, edge_src, edge_dst):
            support = x @ W
            msgs = support[edge_src] * edge_weight[:, None]
            agg = jax.ops.segment_sum(msgs, edge_dst, num_segments=N_NODES)
            return agg + b
        key = jax.random.key(seed)
        ks = jax.random.split(key, 8)
        x = jax.random.normal(ks[0], (N_NODES, NFEAT), dtype=jnp.float32)
        W1 = jax.random.normal(ks[1], (NFEAT, NHID), dtype=jnp.float32) / np.sqrt(NFEAT)
        b1 = jax.random.normal(ks[2], (NHID,), dtype=jnp.float32) * 0.01
        W2 = jax.random.normal(ks[3], (NHID, NHID), dtype=jnp.float32) / np.sqrt(NHID)
        b2 = jax.random.normal(ks[4], (NHID,), dtype=jnp.float32) * 0.01
        edge_weight = jax.random.uniform(ks[5], (N_EDGES,), dtype=jnp.float32)
        edge_src = jax.random.randint(ks[6], (N_EDGES,), 0, N_NODES, dtype=jnp.int32)
        edge_dst = jax.random.randint(ks[7], (N_EDGES,), 0, N_NODES, dtype=jnp.int32)
        return {'x': x, 'W1': W1, 'b1': b1, 'W2': W2, 'b2': b2, 'edge_weight': edge_weight, 'edge_src': edge_src, 'edge_dst': edge_dst}
    _L0_gnn_all = _L0_gnn_setup()
    _L0_gnn_in = {k: v for k, v in _L0_gnn_all.items() if k in ('W1', 'b1', 'W2', 'b2')}
    del _L0_gnn_all

    def _L0_ffn_setup():
        import jax, jax.numpy as jnp
        import numpy as np
        C = 256
        HID = 1024
        E = 8
        TEMP = 1.0
        key = jax.random.key(seed)
        ks = jax.random.split(key, 7)
        x = jax.random.normal(ks[0], (8, 2048, C), dtype=jnp.float32)
        W1 = jax.random.normal(ks[1], (C, HID), dtype=jnp.float32) * 0.02
        b1 = jnp.zeros((HID,), dtype=jnp.float32)
        Wg = jax.random.normal(ks[2], (HID, E), dtype=jnp.float32) * 0.02
        bg = jnp.zeros((E,), dtype=jnp.float32)
        Wd = jax.random.normal(ks[3], (E, HID, C), dtype=jnp.float32) * 0.02
        bd = jnp.zeros((E, C), dtype=jnp.float32)
        return {'x': x, 'W1': W1, 'b1': b1, 'Wg': Wg, 'bg': bg, 'Wd': Wd, 'bd': bd}
    _L0_ffn_all = _L0_ffn_setup()
    _L0_ffn_in = {k: v for k, v in _L0_ffn_all.items() if k in ('W1', 'b1', 'Wg', 'bg', 'Wd', 'bd')}
    del _L0_ffn_all
    return {'x': x, 'src': src, 'dst': dst, 'edge_weight': edge_weight, 'L0_gnn_W1': _L0_gnn_in['W1'], 'L0_gnn_b1': _L0_gnn_in['b1'], 'L0_gnn_W2': _L0_gnn_in['W2'], 'L0_gnn_b2': _L0_gnn_in['b2'], 'L0_ffn_W1': _L0_ffn_in['W1'], 'L0_ffn_b1': _L0_ffn_in['b1'], 'L0_ffn_Wg': _L0_ffn_in['Wg'], 'L0_ffn_bg': _L0_ffn_in['bg'], 'L0_ffn_Wd': _L0_ffn_in['Wd'], 'L0_ffn_bd': _L0_ffn_in['bd']}

def reference(x, src, dst, edge_weight, L0_gnn_W1, L0_gnn_b1, L0_gnn_W2, L0_gnn_b2, L0_ffn_W1, L0_ffn_b1, L0_ffn_Wg, L0_ffn_bg, L0_ffn_Wd, L0_ffn_bd):
    import jax
    import jax.numpy as jnp

    def _L0_gnn_ref(x, W1, b1, W2, b2, edge_weight, edge_src, edge_dst):
        import jax, jax.numpy as jnp
        import numpy as np
        N_NODES = 12500
        N_EDGES = 400000
        NFEAT = 256
        NHID = 256

        def _gcn_layer(x, W, b, edge_weight, edge_src, edge_dst):
            support = x @ W
            msgs = support[edge_src] * edge_weight[:, None]
            agg = jax.ops.segment_sum(msgs, edge_dst, num_segments=N_NODES)
            return agg + b
        h = jax.nn.elu(_gcn_layer(x, W1, b1, edge_weight, edge_src, edge_dst))
        h = jax.nn.elu(_gcn_layer(h, W2, b2, edge_weight, edge_src, edge_dst))
        return h

    def _L0_ffn_ref(x, W1, b1, Wg, bg, Wd, bd):
        import jax, jax.numpy as jnp
        import numpy as np
        C = 256
        HID = 1024
        E = 8
        TEMP = 1.0
        orig_shape = x.shape
        xf = x.reshape(-1, orig_shape[-1])
        H = jax.nn.gelu(xf @ W1 + b1, approximate=False)
        probs = jax.nn.softmax((H @ Wg + bg) / TEMP, axis=-1)
        assign = jnp.argmax(probs, axis=-1)
        out = jnp.zeros_like(xf)
        for e in range(Wd.shape[0]):
            y = H @ Wd[e] + bd[e]
            sel = (assign == e)[:, None]
            out = out + jnp.where(sel, probs[:, e:e + 1] * y, 0.0)
        return out.reshape(orig_shape)
    x = x + _L0_gnn_ref(_layernorm(x, axis=-1), L0_gnn_W1, L0_gnn_b1, L0_gnn_W2, L0_gnn_b2, edge_weight, src, dst)
    x = x + _L0_ffn_ref(_layernorm(x, axis=-1)[None], L0_ffn_W1, L0_ffn_b1, L0_ffn_Wg, L0_ffn_bg, L0_ffn_Wd, L0_ffn_bd)[0]
    return x

_drawn_inputs = setup_inputs


def setup_inputs(seed=0):
    import zlib

    import numpy as np

    out = dict(_drawn_inputs(seed))
    spreads = {'L0_ffn_b1': (0.0, 0.8), 'L0_ffn_bg': (0.0, 0.8), 'L0_ffn_bd': (0.0, 0.8)}
    factors = {'L0_gnn_b1': 5.487, 'L0_gnn_b2': 8.0, 'L0_ffn_W1': 8.0, 'L0_ffn_Wg': 8.0, 'L0_ffn_Wd': 8.0}
    for name, (base, spread) in spreads.items():
        noise = np.random.default_rng([zlib.crc32(name.encode()), seed]).standard_normal(out[name].shape)
        drawn = base * np.exp(spread * noise) if base else spread * noise
        out[name] = jnp.asarray(drawn.astype(out[name].dtype))
    for name, factor in factors.items():
        out[name] = (out[name] * factor).astype(out[name].dtype)
    return out
```

```python
import concourse.bass as bass
from concourse import mybir
from contextlib import ExitStack

P = 128


def bass_gnn_then_routed_ffn(
    nc: bass.Bass,
    x: bass.AP,
    src: bass.AP,
    dst: bass.AP,
    edge_weight: bass.AP,
    gnn_W1: bass.AP,
    gnn_b1: bass.AP,
    gnn_W2: bass.AP,
    gnn_b2: bass.AP,
    ffn_W1: bass.AP,
    ffn_b1: bass.AP,
    ffn_Wg: bass.AP,
    ffn_bg: bass.AP,
    ffn_Wd: bass.AP,
    ffn_bd: bass.AP,
    out: bass.AP,
):
    f32, i32 = mybir.dt.float32, mybir.dt.int32
    ALU, ACT, AX = mybir.AluOpType, mybir.ActivationFunctionType, mybir.AxisListType

    N, C = x.shape
    E = dst.shape[0]
    HID = ffn_W1.shape[1]
    NX = ffn_Wg.shape[1]
    KC = C // P
    KH = HID // P
    T = 4
    GE = T * P
    W = 96
    SLOTS = 4
    ITERS = -(-E // (GE * SLOTS))
    NG = ITERS * SLOTS
    NB = -(-N // P)
    NPAD = NB * P
    AGG = NPAD + W
    GCH = -(-NG // P)
    TBL = NG + 8
    FULL_ROWS = E // GE
    LAST_EDGES = E - FULL_ROWS * GE
    BODY = (GCH - 1) * P
    TAILG = NG - BODY
    PAY = HID + C + 8
    PROB = HID + C
    REG = NPAD + HID
    NT = NB + NX - 1
    NTP = 112
    FAR = float(1 << 22)
    EPS = 1e-5
    KWIN = (N - 1) // W
    assert NX * NPAD < (1 << 22) and REG >= (NT + 1) * P - 0 and TAILG <= 32

    xn_d = nc.dram_tensor("xn_scratch", [N, C], f32, kind="Internal").ap()
    h1_d = nc.dram_tensor("h1_scratch", [NPAD, C], f32, kind="Internal").ap()
    pay_d = nc.dram_tensor("pay_scratch", [NPAD, PAY], f32, kind="Internal").ap()
    list_d = nc.dram_tensor("list_scratch", [NX * REG, 1], i32, kind="Internal").ap()
    gtab_d = nc.dram_tensor("group_scratch", [2, GCH * P], i32, kind="Internal").ap()

    ctx = ExitStack()
    with ctx:
        def sb(name, shape, dt=f32):
            return ctx.enter_context(nc.sbuf_tensor(name, shape, dt))

        def ps(name, shape):
            return ctx.enter_context(nc.psum_tensor(name, shape, f32))

        def sem(name):
            return ctx.enter_context(nc.semaphore(name))

        aggT = sb("aggT", [P, KC, AGG])
        rows = sb("rows", [P, SLOTS, T, C])
        tdst = sb("tdst", [P, T, TBL])
        twgt = sb("twgt", [P, T, TBL])
        tsrc = sb("tsrc", [P, T, TBL])
        idx = sb("idx", [P, SLOTS, T], i32)
        S = sb("S", [P, 2, T, W])
        Sov = sb("Sov", [P, T, W])
        cur = sb("cur", [P, T])
        woff = sb("woff", [P, KWIN + 1])
        regs = sb("regs", [1, NG, 4], i32)
        wg1 = sb("wg1", [P, KC, C])
        wg2 = sb("wg2", [P, KC, C])
        w1 = sb("w1", [P, KC, HID])
        wgate = sb("wgate", [P, KH, NX])
        b1col = sb("b1col", [P, KH])
        brow = sb("brow", [1, 2 * C + NX])
        ident = sb("ident", [P, P])
        ones = sb("ones", [P, P])
        before = sb("before", [P, P])
        iota_w = sb("iota_w", [P, W])
        stats = sb("stats", [P, T, 6])
        mv = sb("mv", [P, T, 2])
        std = sb("std", [P, T])
        rstd = sb("rstd", [P, T])
        nmr = sb("nmr", [P, T])
        stage = sb("stage", [P, 2, KC, P])
        zmin = sb("zmin", [P, 2, C])
        zexp = sb("zexp", [P, 2, C])
        hsum = sb("hsum", [P, 2, C])
        hout = sb("hout", [P, 2, C])
        HT = sb("HT", [P, 2, KH, P])
        pay = sb("pay", [P, 2, PAY])
        xb = rows[:, 0, :, :]
        xnT = rows[:, 1, :, :].rearrange("p t c -> p (t c)")[:, 0:2 * C].rearrange("p (b k n) -> p b k n", b=2, k=KC)
        xn2 = rows[:, 2, :, :]
        hid = sb("hid", [P, KH, P])
        small = sb("small", [P, 16, NX])
        node = sb("node", [P, 2])
        off = sb("off", [P, NX])
        lane = sb("lane", [P, 2])
        col = sb("col", [P, 16])
        place = sb("place", [P, 2], i32)
        nodeid = sb("nodeid", [P, 2], i32)
        prefer = sb("prefer", [P, NX])
        tnum = sb("tnum", [1, NTP])
        fill = sb("fill", [P, NX * REG // P], i32)
        flat = aggT[:, :, :].rearrange("p k n -> p (k n)")
        RW = GCH * GE
        rdst_i = flat[:, 0:RW].bitcast(i32).rearrange("p (c e) -> p c e", c=GCH)
        rsrc_i = flat[:, RW:2 * RW].bitcast(i32).rearrange("p (c e) -> p c e", c=GCH)
        rwgt = flat[:, 2 * RW:3 * RW].rearrange("p (c e) -> p c e", c=GCH)
        rdst = flat[:, 3 * RW:4 * RW].rearrange("p (c e) -> p c e", c=GCH)
        rsrc = flat[:, 4 * RW:5 * RW].rearrange("p (c e) -> p c e", c=GCH)
        rrel = flat[:, 5 * RW:6 * RW].rearrange("p (c e) -> p c e", c=GCH)
        g0 = 6 * RW
        def gvec(n, dt=f32):
            v = flat[:, g0 + n * GCH:g0 + (n + 1) * GCH]
            return v if dt is f32 else v.bitcast(dt)
        def grow(n, dt=f32):
            v = pay[0:1, :, :].rearrange("o b f -> o (b f)")[:, n * GCH * P:(n + 1) * GCH * P]
            return v if dt is f32 else v.bitcast(dt)
        wdk = flat[:, 0:NX * KH * C].rearrange("p (k xc) -> p k xc", k=KH)
        o1 = NX * KH * C
        bd = flat[0:1, o1:o1 + NX * C]
        o2 = o1 + NX * C
        pay2 = flat[:, o2:o2 + 2 * PAY].rearrange("p (b f) -> p b f", b=2)
        o3 = o2 + 2 * PAY
        obuf = flat[:, o3:o3 + 2 * C].rearrange("p (b c) -> p b c", b=2)
        ids = idx[:, 0, 0:2]
        etab = regs[0:1, :, :].rearrange("o g r -> o (g r)")[:, 0:2 * NTP].rearrange("o (r t) -> o r t", r=2)
        erow = hid[0:1, :, :].rearrange("o k n -> o (k n)")[:, 0:8 * NTP].rearrange("o (r t) -> o r t", r=8)
        assert o3 + 2 * C <= KC * AGG and g0 + 8 * GCH <= KC * AGG and 5 * GCH * P <= 2 * PAY

        pA = ps("pA", [P, 2, 512])
        pB = ps("pB", [P, 1024])
        pC = ps("pC", [P, 1024])
        pD = ps("pD", [P, 512])
        pE = ps("pE", [P, 512])

        block = ctx.enter_context(nc.Block())

        s_held = {e.engine: sem(f"held_{n}") for n, e in
                  (("sync", nc.sync), ("pool", nc.gpsimd), ("dve", nc.vector))}
        s_const = sem("constants_ready")
        s_rows_clear = sem("edge_rows_padded")
        s_rows = sem("edge_rows_loaded")
        s_w = sem("weights_loaded")
        s_tchain = sem("dve_table_step")
        s_float = sem("edge_rows_float")
        s_tT = sem("table_transposed")
        s_tcopied = sem("table_copied")
        s_gvec = sem("group_vectors_ready")
        s_gst = sem("group_vectors_stored")
        s_gld = sem("group_rows_loaded")
        s_regs = sem("register_table_ready")
        s_tbl_clear = sem("tables_cleared")
        s_xin = [sem(f"x_loaded_{i}") for i in range(SLOTS)]
        s_xst = [sem(f"xn_stored_{i}") for i in range(SLOTS)]
        s_xtail = sem("x_tail")
        s_ln = sem("dve_layernorm_step")
        s_var = sem("variance_ready")
        s_std = sem("std_ready")
        s_nmr = sem("layernorm_scales_ready")
        s_nd = sem("normalised_by_dve")
        s_na = sem("normalised_by_act")
        s_aggclear = [sem(f"aggT_cleared_{l}") for l in range(2)]
        s_idx = [sem(f"indices_staged_{l}") for l in range(2)]
        s_gath = [[sem(f"rows_gathered_{l}_{i}") for i in range(SLOTS)] for l in range(2)]
        s_S = [sem(f"S_ready_{l}") for l in range(2)]
        s_mm = [sem(f"group_multiplied_{l}") for l in range(2)]
        s_add = [sem(f"group_added_{l}") for l in range(2)]
        s_ovS = [sem(f"overflow_S_ready_{l}") for l in range(2)]
        s_ovmm = [sem(f"overflow_multiplied_{l}") for l in range(2)]
        s_ovadd = [sem(f"overflow_added_{l}") for l in range(2)]
        s_ovc = [sem(f"overflow_window_moved_{l}") for l in range(2)]
        s_stage = [sem(f"block_staged_{l}") for l in range(2)]
        s_z = [sem(f"Z_ready_{l}") for l in range(2)]
        s_zmin = [sem(f"Z_min_ready_{l}") for l in range(2)]
        s_zexp = [sem(f"Z_exp_ready_{l}") for l in range(2)]
        s_hsum = [sem(f"elu_sum_ready_{l}") for l in range(2)]
        s_hout = sem("h1_ready")
        s_h1st = [sem(f"h1_stored_{i}") for i in range(2)]
        s_fill = sem("lists_filled")
        s_xb = [sem(f"x_block_loaded_{i}") for i in range(2)]
        s_node = sem("node_numbers_ready")
        s_blk = sem("dve_block_step")
        s_var2 = sem("block_variance_ready")
        s_std2 = sem("block_std_ready")
        s_xn2 = sem("block_normalised")
        s_xT = sem("block_transposed")
        s_xTc = sem("block_transpose_copied")
        s_hT = sem("hidden_ready")
        s_hb = sem("hidden_biased")
        s_gelu = sem("hidden_activated")
        s_log = sem("logits_ready")
        s_hback = sem("hidden_transposed_back")
        s_payh = sem("payload_hidden_ready")
        s_nmx = sem("negated_max_ready")
        s_gexp = sem("gate_exp_ready")
        s_oh = sem("choice_ready")
        s_rank = sem("ranks_ready")
        s_place = sem("places_ready")
        s_pay = [sem(f"payload_stored_{i}") for i in range(2)]
        s_list = [sem(f"list_scattered_{i}") for i in range(2)]
        s_wd = sem("expert_weights_loaded")
        s_et = sem("dve_expert_table_step")
        s_etr = sem("expert_table_ready")
        s_ids = [sem(f"ids_loaded_{i}") for i in range(2)]
        s_pg = [sem(f"payload_gathered_{i}") for i in range(2)]
        s_eT = sem("expert_tile_transposed")
        s_eTa = sem("expert_tile_copied_by_act")
        s_eTd = sem("expert_tile_copied_by_dve")
        s_y = sem("expert_output_ready")
        s_o = sem("output_tile_ready")
        s_out = [sem(f"output_scattered_{i}") for i in range(2)]

        def need(eng, semaphore, value):
            if isinstance(value, int) and value < 1:
                return
            eng.wait_ge(semaphore, value)

        def hold(eng, semaphore, value):
            if isinstance(value, int) and value < 1:
                return
            eng.wait_ge(semaphore, value)
            if not isinstance(value, int):
                eng.sem_inc(s_held[eng.engine], 1)

        class Steps:

            def __init__(self, eng, semaphore):
                self.eng, self.sem, self.base, self.n = eng, semaphore, 0, 0

            def then(self, ins, own=False):
                self.n += 1
                ins.then_inc(self.sem, 1)
                (hold if own else need)(self.eng, self.sem, self.base + self.n)

        def within(value, low, high):
            return nc.s_assert_within(value, low, high, skip_runtime_bounds_check_because=
                                      "windows end at the group's largest dst, which is below the number of nodes")

        def runs(eng, count):
            yield 0
            with eng.Fori(1, count - 1) as i:
                yield i
            yield count - 1

        LNC = NB // T
        LNI = LNC // SLOTS
        LTAIL = NB - LNC * T
        LAST = N - (NB - 1) * P
        assert LNC == LNI * SLOTS and LTAIL == 2

        @block.sync
        def _(sp):
            sp.wait_ge(s_rows_clear, 3)
            tabs = ((rdst_i, dst), (rsrc_i, src), (rwgt, edge_weight))
            for to, frm in tabs:
                sp.dma_start(to[:, 0:GCH - 1, :],
                             frm[0:BODY * GE].rearrange("(c p e) -> p c e", p=P, e=GE)).then_inc(s_rows, 16)
                sp.dma_start(to[0:FULL_ROWS - BODY, GCH - 1, :],
                             frm[BODY * GE:FULL_ROWS * GE].rearrange("(p e) -> p e", e=GE)).then_inc(s_rows, 16)
                sp.dma_start(to[FULL_ROWS - BODY:FULL_ROWS - BODY + 1, GCH - 1, 0:LAST_EDGES],
                             frm[FULL_ROWS * GE:E].rearrange("(a e) -> a e", a=1)).then_inc(s_rows, 16)

            def x_chunk(c):
                return x[bass.ds(c * (T * P), T * P), :].rearrange("(t p) f -> p t f", p=P)

            def xn_chunk(c):
                return xn_d[bass.ds(c * (T * P), T * P), :].rearrange("(t p) f -> p t f", p=P)

            for c in range(SLOTS - 1):
                sp.dma_start(rows[:, c, :, :], x_chunk(c)).then_inc(s_xin[c], 16)
            sp.wait_ge(s_gvec, 1)
            with nc.allow_non_contiguous_dma(reason="512 values each, once"):
                sp.dma_start(gtab_d[0, :].rearrange("(c p) -> p c", p=P), gvec(7, i32)).then_inc(s_gst, 16)
                sp.dma_start(gtab_d[1, :].rearrange("(c p) -> p c", p=P), gvec(4, i32)).then_inc(s_gst, 16)
            sp.wait_ge(s_gst, 32)
            sp.dma_start(grow(0, i32), gtab_d[0:1, :]).then_inc(s_gld, 16)
            sp.dma_start(grow(1, i32), gtab_d[1:2, :]).then_inc(s_gld, 16)
            for to, frm in ((wg1, gnn_W1), (wg2, gnn_W2), (w1, ffn_W1), (wgate, ffn_Wg)):
                sp.dma_start(to[:, :, :], frm.rearrange("(k p) n -> p k n", p=P)).then_inc(s_w, 16)
            for at, frm in ((0, gnn_b1), (C, gnn_b2), (2 * C, ffn_bg)):
                sp.dma_start(brow[0:1, at:at + frm.shape[0]], frm.rearrange("(a n) -> a n", a=1)).then_inc(s_w, 16)
            with nc.allow_non_contiguous_dma(reason="1024 bias values, once"):
                sp.dma_start(b1col[:, :], ffn_b1.rearrange("(k p) -> p k", p=P)).then_inc(s_w, 16)

            for i in runs(sp, LNI):
                for s in range(SLOTS):
                    c = SLOTS * i + s
                    nxt = c + SLOTS - 1
                    if not isinstance(i, int) or nxt < LNC:
                        need(sp, s_xst[(s - 1) % SLOTS], 16 * (i + 1 if s else i))
                        sp.dma_start(rows[:, (s - 1) % SLOTS, :, :], x_chunk(nxt)).then_inc(s_xin[(s - 1) % SLOTS], 16)
                    sp.wait_ge(s_nd, c + 1)
                    sp.wait_ge(s_na, c + 1)
                    sp.dma_start(xn_chunk(c), rows[:, s, :, :]).then_inc(s_xst[s], 16)
            sp.wait_ge(s_xst[SLOTS - 1], 16 * LNI)
            sp.dma_start(rows[:, SLOTS - 1, 0, :], x[LNC * T * P:(NB - 1) * P, :]).then_inc(s_xtail, 16)
            sp.dma_start(rows[0:LAST, SLOTS - 1, 1, :], x[(NB - 1) * P:N, :]).then_inc(s_xtail, 16)
            sp.wait_ge(s_nd, LNC + 1)
            sp.wait_ge(s_na, LNC + 1)
            sp.dma_start(xn_d[LNC * T * P:(NB - 1) * P, :], rows[:, SLOTS - 1, 0, :]).then_inc(s_xst[SLOTS - 1], 16)
            sp.dma_start(xn_d[(NB - 1) * P:N, :], rows[0:LAST, SLOTS - 1, 1, :]).then_inc(s_xst[SLOTS - 1], 16)

            sp.wait_ge(s_const, 10)
            sp.dma_start(list_d.rearrange("(p n) a -> p (n a)", p=P), fill[:, :]).then_inc(s_fill, 16)

            for i in runs(sp, NB // 2):
                for b2 in range(2):
                    b = 2 * i + b2
                    sp.wait_ge(s_hout, b + 1)
                    sp.dma_start(h1_d[bass.ds(b * P, P), :], hout[:, b2, :]).then_inc(s_h1st[b2], 16)

            sp.wait_ge(s_mm[1], NG)

            def load_x(b, b2):
                sp.dma_start(xb[:, b2, :], x[bass.ds(b * P, P), :]).then_inc(s_xb[b2], 16)

            def store_payload(b, b2):
                hold(sp, s_payh, 2 * b + 2)
                sp.wait_ge(s_place, b + 1)
                sp.dma_start(pay_d[bass.ds(b * P, P), :], pay[:, b2, :]).then_inc(s_pay[b2], 16)

            load_x(0, 0)
            load_x(1, 1)
            with sp.Fori(0, NB // 2 - 2) as i:
                for b2 in range(2):
                    store_payload(2 * i + b2, b2)
                    load_x(2 * i + b2 + 2, b2)
            store_payload(NB - 4, 0)
            load_x(NB - 2, 0)
            store_payload(NB - 3, 1)
            sp.dma_start(xb[0:LAST, 1, :], x[(NB - 1) * P:N, :]).then_inc(s_xb[1], 16)
            for b2 in range(2):
                store_payload(NB - 2 + b2, b2)

            sp.wait_ge(s_stage[1], NB)
            for k in range(KH):
                sp.dma_start(wdk[:, k, :].rearrange("p (x c) -> p x c", x=NX),
                             ffn_Wd[:, k * P:(k + 1) * P, :].rearrange("x p c -> p x c")).then_inc(s_wd, 16)
            sp.dma_start(bd, ffn_bd.rearrange("x (a c) -> a (x c)", a=1)).then_inc(s_wd, 16)

            def load_ids(t, b2):
                at = sp.value_load(etab[0:1, 1, bass.ds(t, 1)], min_val=0, max_val=NX * REG - P)
                sp.dma_start(ids[:, b2:b2 + 1], list_d[bass.ds(at, P), :]).then_inc(s_ids[b2], 16)

            sp.wait_ge(s_list[0], 16 * (NB // 2))
            sp.wait_ge(s_list[1], 16 * (NB // 2))
            sp.wait_ge(s_etr, 1)
            load_ids(0, 0)
            load_ids(1, 1)
            with sp.Fori(0, NTP // 2 - 1) as i:
                for b2 in range(2):
                    sp.wait_ge(s_out[b2], 16 * (i + 1))
                    load_ids(2 * i + 2 + b2, b2)
            for b2 in range(2):
                sp.wait_ge(s_out[b2], 16 * (NTP // 2))

        @block.gpsimd
        def _(pool):
            pool.memset(rdst_i[0:TAILG, GCH - 1, :], N - 1).then_inc(s_rows_clear, 1)
            pool.memset(rsrc_i[0:TAILG, GCH - 1, :], 0).then_inc(s_rows_clear, 1)
            pool.memset(rwgt[0:TAILG, GCH - 1, :], 0.0).then_inc(s_rows_clear, 1)
            for t in (tdst, twgt, tsrc):
                pool.memset(t[:, :, NG:TBL], 0.0).then_inc(s_tbl_clear, 1)
            pool.memset(ones[:, :], 1.0).then_inc(s_const, 1)
            pool.wait_ge(s_const, 1)
            pool.affine_select(out=ident[:, :], in_=ones[:, :], compare_op=ALU.is_equal, fill=0.0, base=0,
                               pattern=[[-1, P]], channel_multiplier=1).then_inc(s_const, 1)
            pool.affine_select(out=before[:, :], in_=ones[:, :], compare_op=ALU.is_gt, fill=0.0, base=0,
                               pattern=[[1, P]], channel_multiplier=-1).then_inc(s_const, 1)
            pool.iota(iota_w[:, :], [[1, W]], base=0, channel_multiplier=0,
                      allow_small_or_imprecise_dtypes=True).then_inc(s_const, 1)
            pool.iota(lane[:, :], [[0, 2]], base=0, channel_multiplier=1,
                      allow_small_or_imprecise_dtypes=True).then_inc(s_const, 1)
            pool.iota(off[:, :], [[REG, NX]], base=0, channel_multiplier=0,
                      allow_small_or_imprecise_dtypes=True).then_inc(s_const, 1)
            pool.memset(fill[:, :], N).then_inc(s_const, 1)
            pool.iota(woff[:, :], [[W, KWIN + 1]], base=0, channel_multiplier=0,
                      allow_small_or_imprecise_dtypes=True).then_inc(s_const, 1)
            pool.iota(prefer[:, :], [[-1, NX]], base=NX, channel_multiplier=0,
                      allow_small_or_imprecise_dtypes=True).then_inc(s_const, 1)
            pool.iota(tnum[:, :], [[1, NTP]], base=0, channel_multiplier=0,
                      allow_small_or_imprecise_dtypes=True).then_inc(s_const, 1)

            for layer, table in ((0, xn_d), (1, h1_d)):
                if layer == 0:
                    pool.wait_ge(s_tcopied, 3 * GCH)
                    pool.wait_ge(s_gst, 32)
                else:
                    pool.wait_ge(s_stage[0], NB)
                pool.memset(aggT[:, :, :], 0.0).then_inc(s_aggclear[layer], 1)
                if layer == 0:
                    for s in range(SLOTS - 1):
                        pool.wait_ge(s_xst[s], 16 * LNI)
                    pool.wait_ge(s_xst[SLOTS - 1], 16 * (LNI + 2))
                else:
                    for b2 in range(2):
                        pool.wait_ge(s_h1st[b2], 16 * (NB // 2))
                for i in runs(pool, ITERS):
                    for s in range(SLOTS):
                        g = SLOTS * i + s
                        hold(pool, s_idx[layer], g + 1)
                        hold(pool, s_mm[layer], g - (SLOTS - 1))
                        for t in range(T):
                            pool.indirect_dma_start(rows[:, s, t, :], None, table,
                                                    bass.IndirectOffsetOnAxis(idx[:, s, t:t + 1], 0))\
                                .then_inc(s_gath[layer][s], 16)

            pool.wait_ge(s_fill, 16)
            with pool.Fori(0, NB // 2) as i:
                for b2 in range(2):
                    hold(pool, s_place, 2 * i + b2 + 1)
                    pool.indirect_dma_start(list_d, bass.IndirectOffsetOnAxis(place[:, b2:b2 + 1], 0),
                                            nodeid[:, b2:b2 + 1], None,
                                            bounds_check=NX * REG - 1, oob_is_err=False).then_inc(s_list[b2], 16)

            for b2 in range(2):
                pool.wait_ge(s_pay[b2], 16 * (NB // 2))
            def gather(t, i, b2):
                hold(pool, s_ids[b2], 16 * (i + 1))
                pool.indirect_dma_start(pay2[:, b2, :], None, pay_d,
                                        bass.IndirectOffsetOnAxis(ids[:, b2:b2 + 1], 0)).then_inc(s_pg[b2], 16)
            gather(0, 0, 0)
            gather(1, 0, 1)
            with pool.Fori(0, NTP // 2 - 1) as i:
                for b2 in range(2):
                    t = 2 * i + b2
                    hold(pool, s_o, t + 1)
                    pool.indirect_dma_start(out, bass.IndirectOffsetOnAxis(ids[:, b2:b2 + 1], 0), obuf[:, b2, :],
                                            None, bounds_check=N - 1, oob_is_err=False).then_inc(s_out[b2], 16)
                for b2 in range(2):
                    gather(2 * i + 2 + b2, i + 1, b2)
            for b2 in range(2):
                pool.wait_ge(s_o, NTP - 1 + b2)
                pool.indirect_dma_start(out, bass.IndirectOffsetOnAxis(ids[:, b2:b2 + 1], 0), obuf[:, b2, :],
                                        None, bounds_check=N - 1, oob_is_err=False).then_inc(s_out[b2], 16)

        @block.scalar
        def _(act):
            def ln(c, s, n):
                act.wait_ge(s_var, c + 1)
                act.activation(std[:, 0:n], mv[:, 0:n, 1], ACT.Sqrt, bias=eps_col).then_inc(s_std, 1)
                act.wait_ge(s_nmr, c + 1)
                half = n // 2
                for t in range(half, n):
                    last = act.activation(rows[:, s, t, :], rows[:, s, t, :], ACT.Identity,
                                          bias=nmr[:, t:t + 1], scale=rstd[:, t:t + 1])
                last.then_inc(s_na, 1)

            eps_col = col[:, 15:16]
            for n in range(3 * GCH):
                c = n % GCH
                cnt = P if c < GCH - 1 else TAILG
                act.wait_ge(s_tT, n + 1)
                act.activation((tdst, tsrc, twgt)[n // GCH][:, :, c * P:c * P + cnt],
                               pB[:, (n % 2) * 512:(n % 2 + 1) * 512].rearrange("p (t g) -> p t g", t=T)[:, :, 0:cnt],
                               ACT.Copy).then_inc(s_tcopied, 1)

            act.wait_ge(s_ln, 1)
            for i in runs(act, LNI):
                for s in range(SLOTS):
                    ln(SLOTS * i + s, s, T)
            ln(LNC, SLOTS - 1, LTAIL)

            for layer in range(2):
                def stage_idx(g, s):
                    act.activation(idx[:, s, :], tsrc[:, :, bass.ds(g, 1)].rearrange("p t g -> p (t g)"),
                                   ACT.Copy).then_inc(s_idx[layer], 1)

                for s in range(SLOTS):
                    if layer:
                        act.wait_ge(s_gath[0][s], 16 * T * ITERS)
                    stage_idx(s, s)
                with act.Fori(0, ITERS - 1) as i:
                    for s in range(SLOTS):
                        act.wait_ge(s_gath[layer][s], 16 * T * (i + 1))
                        stage_idx(SLOTS * i + SLOTS + s, s)

                act.wait_ge(s_add[layer], NG)

                def elu(b, b2):
                    act.wait_ge(s_zmin[layer], b + 1)
                    act.activation(zexp[:, b2, :], zmin[:, b2, :], ACT.Exp).then_inc(s_zexp[layer], 1)

                def put_stage(b, b2):
                    need(act, s_z[layer], b - 1)
                    act.activation(stage[:, b2, :, :], aggT[:, :, bass.ds(b * P, P)], ACT.Copy)\
                       .then_inc(s_stage[layer], 1)

                def h1(i, b, b2):
                    act.wait_ge(s_hsum[layer], b + 1)
                    need(act, s_h1st[b2], 16 * i)
                    act.activation(hout[:, b2, :], hsum[:, b2, :], ACT.Copy, bias=-1.0).then_inc(s_hout, 1)

                if layer == 0:
                    put_stage(0, 0)
                    for i in runs(act, NB // 2):
                        for b2 in range(2):
                            b = 2 * i + b2
                            if not isinstance(i, int) or b + 1 < NB:
                                put_stage(b + 1, 1 - b2)
                            elu(b, b2)
                            h1(i, b, b2)
                else:
                    for i in runs(act, NB // 2):
                        for b2 in range(2):
                            b = 2 * i + b2
                            put_stage(b, b2)
                            elu(b, b2)
                            act.wait_ge(s_var2, b + 1)
                            act.activation(col[:, 8:9], col[:, 1:2], ACT.Sqrt, bias=eps_col).then_inc(s_std2, 1)
                            act.wait_ge(s_hb, b + 1)
                            act.activation(HT[:, b2, :, :], hid[:, :, :], ACT.Gelu).then_inc(s_gelu, 1)
                            act.wait_ge(s_nmx, b + 1)
                            act.activation(small[:, 0, :], pE[:, 0:NX], ACT.Exp, bias=col[:, 3:4],
                                           accum_out=col[:, 4:5]).then_inc(s_gexp, 1)
                            act.wait_ge(s_hback, b + 1)
                            need(act, s_pay[b2], 16 * i)
                            act.activation(pay[:, b2, 0:HID // 2], pC[:, 0:HID // 2], ACT.Copy).then_inc(s_payh, 1)

            with act.Fori(0, NTP // 2) as i:
                for b2 in range(2):
                    t = 2 * i + b2
                    act.wait_ge(s_eT, t + 1)
                    act.activation(HT[:, b2, 0:KH // 2, :], pB[:, 0:512].rearrange("p (k n) -> p k n", k=KH // 2),
                                   ACT.Copy).then_inc(s_eTa, 1)

        @block.vector
        def _(dve):
            v = nc.vector
            lnc = Steps(dve, s_ln)
            lnc.then(v.memset(col[:, 15:16], EPS))

            tc = Steps(dve, s_tchain)
            dve.wait_ge(s_rows, 9 * 16)
            parts = ((P, slice(0, GCH - 1)), (TAILG, slice(GCH - 1, GCH)))
            for n, c in parts:
                v.tensor_copy(rsrc[0:n, c, :], rsrc_i[0:n, c, :]).then_inc(s_float, 1)
                tc.then(v.tensor_copy(rdst[0:n, c, :], rdst_i[0:n, c, :]))
            LO, HI, D, Q = gvec(0), gvec(1), gvec(2), gvec(3)
            LOi, Di, Qi, NVi = gvec(4, i32), gvec(5, i32), gvec(6, i32), gvec(7, i32)
            tc.then(v.memset(flat[:, g0:g0 + 2 * GCH], 0.0))
            for n, c in parts:
                v.tensor_reduce(LO[0:n, c], rdst[0:n, c, :], axis=AX.X, op=ALU.min)
                tc.then(v.tensor_reduce(HI[0:n, c], rdst[0:n, c, :], axis=AX.X, op=ALU.max))
            for c in range(GCH):
                n = P if c < GCH - 1 else TAILG
                v.tensor_scalar(rrel[0:n, c, :], rdst[0:n, c, :], LO[0:n, c:c + 1], None, ALU.subtract)\
                 .then_inc(s_float, 1)
            assert W == 96
            tc.then(v.tensor_tensor(D, HI, LO, ALU.subtract))
            tc.then(v.tensor_copy(Di, D))
            tc.then(v.tensor_scalar(Qi, Di, 5, None, ALU.arith_shift_right))
            tc.then(v.tensor_copy(Q, Qi))
            tc.then(v.tensor_scalar(D, Q, 21846.0, None, ALU.mult))
            tc.then(v.tensor_copy(Di, D))
            tc.then(v.tensor_scalar(NVi, Di, 16, None, ALU.arith_shift_right))
            v.tensor_copy(LOi, LO).then_inc(s_gvec, 1)
            def ln(c, s, n, first=False):
                for t in range(n):
                    last = v.bn_stats(stats[:, t, :], rows[:, s, t, :])
                lnc.then(last, own=True)
                for t in range(n):
                    last = v.bn_aggr(mv[:, t, :], stats[:, t, :])
                last.then_inc(s_var, 1)
                dve.wait_ge(s_std, c + 1)
                need(dve, s_na, c)
                lnc.then(v.reciprocal(rstd[:, 0:n], std[:, 0:n]))
                v.scalar_tensor_tensor(out=nmr[:, 0:n], in0=mv[:, 0:n, 0], scalar=-1.0, in1=rstd[:, 0:n],
                                       op0=ALU.mult, op1=ALU.mult).then_inc(s_nmr, 1)
                for t in range(n // 2):
                    last = v.tensor_scalar(rows[:, s, t, :], rows[:, s, t, :], mv[:, t, 0:1], rstd[:, t:t + 1],
                                           ALU.subtract, ALU.mult)
                last.then_inc(s_nd, 1)

            def ln_base(i):
                lnc.base, lnc.n = 1 + 2 * SLOTS * i, 0

            for i in runs(dve, LNI):
                ln_base(i)
                for s in range(SLOTS):
                    dve.wait_ge(s_xin[s], 16 * (i + 1))
                    ln(SLOTS * i + s, s, T)
            lnc.base, lnc.n = 1 + 2 * LNC, 0
            dve.wait_ge(s_xtail, 32)
            ln(LNC, SLOTS - 1, LTAIL)

            dve.wait_ge(s_gld, 32)
            NVr, LOr, NVf, INC, STA = grow(0, i32), grow(1, i32), grow(2), grow(3), grow(4)
            tc.then(v.tensor_copy(NVf, NVr))
            tc.then(v.tensor_tensor_scan(INC, NVf, NVf, 0.0, ALU.add, ALU.bypass))
            tc.then(v.tensor_tensor(STA, INC, NVf, ALU.subtract))
            for r, frm in ((0, STA), (1, INC), (2, LOr), (3, LOr)):
                last = v.tensor_copy(regs[0:1, :, r], frm[:, 0:NG])
            last.then_inc(s_regs, 1)

            def build_S(layer, g, half):
                need(dve, s_mm[layer], g - 1)
                for t in range(T):
                    last = v.tensor_scalar(S[:, half, t, :], iota_w[:, :], tdst[:, t, bass.ds(g, 1)],
                                           twgt[:, t, bass.ds(g, 1)], ALU.is_equal, ALU.mult)
                last.then_inc(s_S[layer], 1)

            def add_group(layer, g, half):
                ws = dve.value_load(regs[0:1, bass.ds(g, 1), 0], min_val=0, max_val=NG * P)
                we = dve.value_load(regs[0:1, bass.ds(g, 1), 1], min_val=0, max_val=NG * P)
                base = dve.value_load(regs[0:1, bass.ds(g, 1), 2], min_val=0, max_val=N - 1)
                hold(dve, s_add[layer], g)
                with dve.If(ws < we):
                    with dve.Fori(ws, we) as w:
                        k = within(w - ws + 1, 1, KWIN)
                        v.tensor_scalar(cur[:, :], tdst[:, :, bass.ds(g, 1)].rearrange("p t g -> p (t g)"),
                                        woff[:, bass.ds(k, 1)], None, ALU.subtract).then_inc(s_ovc[layer], 1)
                        dve.wait_ge(s_ovc[layer], w + 1)
                        for t in range(T):
                            last = v.tensor_scalar(Sov[:, t, :], iota_w[:, :], cur[:, t:t + 1],
                                                   twgt[:, t, bass.ds(g, 1)], ALU.is_equal, ALU.mult)
                        last.then_inc(s_ovS[layer], 1)
                        dve.wait_ge(s_ovmm[layer], w + 1)
                        at = within(base + k * W, 0, N - 1)
                        far = aggT[:, :, bass.ds(at, W)]
                        v.tensor_tensor(far, far, pB[:, 0:KC * W].rearrange("p (k n) -> p k n", k=KC), ALU.add)\
                         .then_inc(s_ovadd[layer], 1)
                        hold(dve, s_ovadd[layer], w + 1)
                dve.wait_ge(s_mm[layer], g + 1)
                to = aggT[:, :, bass.ds(base, W)]
                v.tensor_tensor(to, to, pA[:, half, 0:KC * W].rearrange("p (k n) -> p k n", k=KC), ALU.add)\
                 .then_inc(s_add[layer], 1)

            bc0 = Steps(dve, s_node)
            dve.wait_ge(s_const, 10)
            dve.wait_ge(s_tcopied, 3 * GCH)
            dve.wait_ge(s_tbl_clear, 3)
            dve.wait_ge(s_regs, 1)
            bc0.then(v.tensor_copy(node[:, :], lane[:, :]))
            bc0.then(v.memset(pay[:, :, PROB:PAY], 0.0))

            for layer in range(2):
                dve.wait_ge(s_aggclear[layer], 1)
                build_S(layer, 0, 0)
                for i in runs(dve, ITERS):
                    for s in range(SLOTS):
                        g = SLOTS * i + s
                        if not isinstance(i, int) or g + 1 < NG:
                            build_S(layer, g + 1, (s + 1) % 2)
                        add_group(layer, g, s % 2)

                def elu_sum(b, b2):
                    dve.wait_ge(s_z[layer], b + 1)
                    need(dve, s_zexp[layer], b - 1)
                    v.tensor_scalar(zmin[:, b2, :], pA[:, b2, 0:C], 0.0, None, ALU.min).then_inc(s_zmin[layer], 1)
                    dve.wait_ge(s_zexp[layer], b + 1)
                    return v.scalar_tensor_tensor(out=hsum[:, b2, :], in0=pA[:, b2, 0:C], scalar=0.0,
                                                  in1=zexp[:, b2, :], op0=ALU.max, op1=ALU.add)

                if layer == 0:
                    for i in runs(dve, NB // 2):
                        for b2 in range(2):
                            b = 2 * i + b2
                            need(dve, s_hout, b - 1)
                            elu_sum(b, b2).then_inc(s_hsum[layer], 1)

            def x1_part(i, b, b2):
                elu_sum(b, b2).then_inc(s_hsum[1], 1)
                dve.wait_ge(s_hsum[1], b + 1)
                dve.wait_ge(s_xb[b2], 16 * (i + 1))
                need(dve, s_pay[b2], 16 * i)
                x1 = pay[:, b2, HID:HID + C]
                bc.then(v.scalar_tensor_tensor(out=x1, in0=hsum[:, b2, :], scalar=-1.0, in1=xb[:, b2, :],
                                               op0=ALU.add, op1=ALU.add))
                bc.then(v.bn_stats(stats[:, 0, :], x1), own=True)
                v.bn_aggr(col[:, 0:2], stats[:, 0, :]).then_inc(s_var2, 1)
                dve.wait_ge(s_std2, b + 1)
                bc.then(v.reciprocal(col[:, 2:3], col[:, 8:9]))
                need(dve, s_xT, b - 1)
                v.tensor_scalar(xn2[:, b2, :], x1, col[:, 0:1], col[:, 2:3], ALU.subtract, ALU.mult)\
                 .then_inc(s_xn2, 1)
                dve.wait_ge(s_xT, b + 1)
                v.tensor_copy(xnT[:, b2, :, :], pD[:, 0:C].rearrange("p (k n) -> p k n", k=KC)).then_inc(s_xTc, 1)

            def hidden_part(b):
                dve.wait_ge(s_hT, b + 1)
                need(dve, s_gelu, b)
                v.tensor_tensor(hid[:, :, :], pB[:, :].rearrange("p (k n) -> p k n", k=KH),
                                b1col[:, :].unsqueeze(2).to_broadcast([P, KH, P]), ALU.add).then_inc(s_hb, 1)

            def gate_part(i, b, b2):
                dve.wait_ge(s_log, b + 1)
                bc.then(v.tensor_reduce(col[:, 5:6], pE[:, 0:NX], axis=AX.X, op=ALU.max))
                v.tensor_scalar(col[:, 3:4], col[:, 5:6], -1.0, None, ALU.mult).then_inc(s_nmx, 1)
                dve.wait_ge(s_hback, b + 1)
                v.tensor_copy(pay[:, b2, HID // 2:HID], pC[:, HID // 2:HID]).then_inc(s_payh, 1)
                dve.wait_ge(s_gexp, b + 1)
                e, sc, oh, a, oa = (small[:, n, :] for n in range(5))
                v.tensor_reduce(col[:, 6:7], e, axis=AX.X, op=ALU.max)
                bc.then(v.reciprocal(col[:, 7:8], col[:, 4:5]))
                v.tensor_scalar(pay[:, b2, PROB:PROB + 1], col[:, 6:7], col[:, 7:8], None, ALU.mult)
                bc.then(v.scalar_tensor_tensor(out=sc, in0=e, scalar=col[:, 6:7], in1=prefer[:, :],
                                               op0=ALU.is_equal, op1=ALU.mult))
                bc.then(v.tensor_reduce(col[:, 9:10], sc, axis=AX.X, op=ALU.max))
                bc.then(v.tensor_scalar(col[:, 10:11], node[:, 0:1], float(N), None, ALU.is_lt))
                v.tensor_scalar(oh, sc, col[:, 9:10], col[:, 10:11], ALU.is_equal, ALU.mult).then_inc(s_oh, 1)
                bc.then(v.tensor_scalar(col[:, 11:12], col[:, 10:11], -FAR, FAR, ALU.mult, ALU.add))
                dve.wait_ge(s_rank, b + 1)
                need(dve, s_place, b)
                bc.then(v.tensor_tensor(a, pE[:, NX:2 * NX], off[:, :], ALU.add))
                bc.then(v.tensor_tensor(oa, a, oh, ALU.mult))
                bc.then(v.tensor_reduce(col[:, 12:13], oa, axis=AX.X, op=ALU.add))
                need(dve, s_list[b2], 16 * i)
                v.tensor_scalar(place[:, b2:b2 + 1], col[:, 12:13], col[:, 11:12], None, ALU.add)
                v.tensor_copy(nodeid[:, b2:b2 + 1], node[:, 0:1])
                v.tensor_scalar(node[:, 0:1], node[:, 0:1], float(P), None, ALU.add)
                v.tensor_tensor(off[:, :], off[:, :], pE[:, 2 * NX:3 * NX], ALU.add).then_inc(s_place, 1)

            bc = Steps(dve, s_blk)
            PER = 12
            for i in runs(dve, NB // 2):
                for b2 in range(2):
                    b = 2 * i + b2
                    bc.base, bc.n = PER * b, 0
                    x1_part(i, b, b2)
                    hidden_part(b)
                    gate_part(i, b, b2)
                    assert bc.n == PER, bc.n

            et = Steps(dve, s_et)
            dve.wait_ge(s_place, NB)
            n_e, tiles, ends, starts = (small[0:1, n, :] for n in range(5, 9))
            ti = small[0:1, 9, :].bitcast(i32)
            tj = small[0:1, 10, :].bitcast(i32)
            first = small[0:1, 11, :]
            et.then(v.tensor_scalar(first, prefer[0:1, :], -float(REG), float(REG * NX), ALU.mult, ALU.add))
            et.then(v.tensor_tensor(n_e, off[0:1, :], first, ALU.subtract))
            et.then(v.tensor_scalar(n_e, n_e, float(P - 1), None, ALU.add))
            et.then(v.tensor_copy(ti, n_e))
            et.then(v.tensor_scalar(tj, ti, 7, None, ALU.arith_shift_right))
            et.then(v.tensor_copy(tiles, tj))
            et.then(v.tensor_tensor_scan(ends, tiles, tiles, 0.0, ALU.add, ALU.bypass))
            et.then(v.tensor_tensor(starts, ends, tiles, ALU.subtract))
            ex, at, tmp = erow[0:1, 0, :], erow[0:1, 1, :], erow[0:1, 2, :]
            et.then(v.memset(erow[0:1, 0:2, :], 0.0))
            for e in range(1, NX):
                et.then(v.tensor_scalar(tmp, tnum[:, :], starts[0:1, e:e + 1], None, ALU.is_ge))
                et.then(v.tensor_tensor(ex, ex, tmp, ALU.add))
                et.then(v.scalar_tensor_tensor(out=at, in0=tmp, scalar=starts[0:1, e:e + 1], in1=at,
                                               op0=ALU.mult, op1=ALU.max))
            et.then(v.tensor_tensor(tmp, tnum[:, :], at, ALU.subtract))
            et.then(v.tensor_scalar(tmp, tmp, float(P), None, ALU.mult))
            et.then(v.scalar_tensor_tensor(out=at, in0=ex, scalar=float(REG), in1=tmp, op0=ALU.mult, op1=ALU.add))
            v.tensor_scalar(etab[0:1, 0, :], ex, float(C), None, ALU.mult)
            v.tensor_copy(etab[0:1, 1, :], at).then_inc(s_etr, 1)

            with dve.Fori(0, NTP // 2) as i:
                for b2 in range(2):
                    t = 2 * i + b2
                    dve.wait_ge(s_eT, t + 1)
                    v.tensor_copy(HT[:, b2, KH // 2:KH, :],
                                  pB[:, 512:1024].rearrange("p (k n) -> p k n", k=KH // 2)).then_inc(s_eTd, 1)
                    dve.wait_ge(s_y, t + 1)
                    v.scalar_tensor_tensor(out=obuf[:, b2, :], in0=pA[:, b2, 0:C], scalar=pay2[:, b2, PROB:PROB + 1],
                                           in1=pay2[:, b2, HID:HID + C], op0=ALU.mult, op1=ALU.add).then_inc(s_o, 1)

        @block.tensor
        def _(pe):
            mm = nc.tensor.matmul
            pe.wait_ge(s_const, 2)
            n = 0
            for table, want in ((rrel, None), (rsrc, None), (rwgt, None)):
                for c in range(GCH):
                    cnt = P if c < GCH - 1 else TAILG
                    if n == 0:
                        pe.wait_ge(s_float, 2 + GCH)
                        pe.wait_ge(s_rows, 9 * 16)
                    need(pe, s_tcopied, n - 1)
                    for t in range(T):
                        at = (n % 2) * 512 + t * P
                        last = nc.tensor.transpose(pB[:, at:at + cnt], table[0:cnt, c, t * P:(t + 1) * P],
                                                   ident[0:cnt, 0:cnt])
                    last.then_inc(s_tT, 1)
                    n += 1
            pe.wait_ge(s_tcopied, 3 * GCH)
            pe.wait_ge(s_regs, 1)

            def products(layer, slot, Sx, to, semaphore):
                for k in range(KC):
                    for t in range(T):
                        last = mm(to[:, k * W:(k + 1) * W], rows[:, slot, t, k * P:(k + 1) * P], Sx[:, t, :],
                                  start=(t == 0), stop=(t == T - 1))
                last.then_inc(semaphore, 1)

            for layer in range(2):
                for i in runs(pe, ITERS):
                    for s in range(SLOTS):
                        g = SLOTS * i + s
                        ws = pe.value_load(regs[0:1, bass.ds(g, 1), 0], min_val=0, max_val=NG * P)
                        we = pe.value_load(regs[0:1, bass.ds(g, 1), 1], min_val=0, max_val=NG * P)
                        pe.wait_ge(s_gath[layer][s], 16 * T * (i + 1))
                        with pe.If(ws < we):
                            with pe.Fori(ws, we) as w:
                                pe.wait_ge(s_ovS[layer], w + 1)
                                products(layer, s, Sov, pB, s_ovmm[layer])
                        pe.wait_ge(s_S[layer], g + 1)
                        need(pe, s_add[layer], g - 1)
                        products(layer, s, S[:, s % 2, :, :], pA[:, s % 2, :], s_mm[layer])

                pe.wait_ge(s_add[layer], NG)
                wg, bat = (wg1, 0) if layer == 0 else (wg2, C)
                if layer == 0:
                    pe.wait_ge(s_w, 8 * 16)

                def z_part(b, b2):
                    pe.wait_ge(s_stage[layer], b + 1)
                    need(pe, s_hsum[layer], b - 1)
                    mm(pA[:, b2, 0:C], ones[0:1, :], brow[0:1, bat:bat + C], start=True, stop=False)
                    for k in range(KC):
                        last = mm(pA[:, b2, 0:C], stage[:, b2, k, :], wg[:, k, :], start=False, stop=(k == KC - 1))
                    last.then_inc(s_z[layer], 1)

                if layer == 0:
                    for i in runs(pe, NB // 2):
                        for b2 in range(2):
                            z_part(2 * i + b2, b2)

            for i in runs(pe, NB // 2):
                for b2 in range(2):
                    b = 2 * i + b2
                    z_part(b, b2)
                    pe.wait_ge(s_xn2, b + 1)
                    need(pe, s_xTc, b)
                    for k in range(KC):
                        last = nc.tensor.transpose(pD[:, k * P:(k + 1) * P], xn2[:, b2, k * P:(k + 1) * P], ident[:, :])
                    last.then_inc(s_xT, 1)
                    pe.wait_ge(s_xTc, b + 1)
                    need(pe, s_hb, b)
                    for m in range(KH):
                        for k in range(KC):
                            last = mm(pB[:, m * P:(m + 1) * P], w1[:, k, m * P:(m + 1) * P], xnT[:, b2, k, :],
                                      start=(k == 0), stop=(k == KC - 1))
                    last.then_inc(s_hT, 1)
                    pe.wait_ge(s_gelu, b + 1)
                    need(pe, s_place, b)
                    mm(pE[:, 0:NX], ones[0:1, :], brow[0:1, 2 * C:2 * C + NX], start=True, stop=False)
                    for m in range(KH):
                        last = mm(pE[:, 0:NX], HT[:, b2, m, :], wgate[:, m, :], start=False, stop=(m == KH - 1))
                    last.then_inc(s_log, 1)
                    need(pe, s_payh, 2 * b)
                    for m in range(KH):
                        last = nc.tensor.transpose(pC[:, m * P:(m + 1) * P], HT[:, b2, m, :], ident[:, :])
                    last.then_inc(s_hback, 1)
                    pe.wait_ge(s_oh, b + 1)
                    mm(pE[:, NX:2 * NX], before[:, :], small[:, 2, :], start=True, stop=True)
                    mm(pE[:, 2 * NX:3 * NX], ones[:, :], small[:, 2, :], start=True, stop=True).then_inc(s_rank, 1)

            pe.wait_ge(s_wd, 16 * (KH + 1))
            pe.wait_ge(s_etr, 1)
            with pe.Fori(0, NTP // 2) as i:
                for b2 in range(2):
                    t = 2 * i + b2
                    ec = pe.value_load(etab[0:1, 0, bass.ds(t, 1)], min_val=0, max_val=(NX - 1) * C)
                    pe.wait_ge(s_pg[b2], 16 * (i + 1))
                    for m in range(KH):
                        last = nc.tensor.transpose(pB[:, m * P:(m + 1) * P], pay2[:, b2, m * P:(m + 1) * P], ident[:, :])
                    last.then_inc(s_eT, 1)
                    pe.wait_ge(s_eTa, t + 1)
                    pe.wait_ge(s_eTd, t + 1)
                    mm(pA[:, b2, 0:C], ones[0:1, :], bd[0:1, bass.ds(ec, C)], start=True, stop=False)
                    for m in range(KH):
                        last = mm(pA[:, b2, 0:C], HT[:, b2, m, :], wdk[:, m, bass.ds(ec, C)],
                                  start=False, stop=(m == KH - 1))
                    last.then_inc(s_y, 1)


_INS = ['x', 'src', 'dst', 'edge_weight', 'L0_gnn_W1', 'L0_gnn_b1', 'L0_gnn_W2', 'L0_gnn_b2',
        'L0_ffn_W1', 'L0_ffn_b1', 'L0_ffn_Wg', 'L0_ffn_bg', 'L0_ffn_Wd', 'L0_ffn_bd']


def kernel(**inputs):
    import numpy as _np
    import concourse.bacc as _bacc
    from concourse import mybir as _mybir
    from concourse.bass_utils import run_bass_kernel_spmd as _run

    nc = _bacc.Bacc("TRN2", target_bir_lowering=False, num_devices=1)
    arrays, args = {}, []
    for name in _INS:
        a = _np.ascontiguousarray(inputs[name])
        arrays[f"in_{name}_dram"] = a
        args.append(nc.dram_tensor(f"in_{name}_dram", a.shape, _mybir.dt.from_np(a.dtype), kind="ExternalInput").ap())
    args.append(nc.dram_tensor("out_0_dram", inputs['x'].shape, _mybir.dt.float32, kind="ExternalOutput").ap())
    bass_gnn_then_routed_ffn(nc, *args)
    nc.compile()
    r = _run(nc, [arrays], core_ids=[0])
    return r.results[0]["out_0_dram"]
```

```python
import concourse.bass as bass
from concourse import mybir
from contextlib import ExitStack

P = 128


def bass_gnn_then_routed_ffn(
    nc: bass.Bass,
    x: bass.AP,
    src: bass.AP,
    dst: bass.AP,
    edge_weight: bass.AP,
    gnn_W1: bass.AP,
    gnn_b1: bass.AP,
    gnn_W2: bass.AP,
    gnn_b2: bass.AP,
    ffn_W1: bass.AP,
    ffn_b1: bass.AP,
    ffn_Wg: bass.AP,
    ffn_bg: bass.AP,
    ffn_Wd: bass.AP,
    ffn_bd: bass.AP,
    out: bass.AP,
):
    f32, i32 = mybir.dt.float32, mybir.dt.int32
    ALU, ACT, AX = mybir.AluOpType, mybir.ActivationFunctionType, mybir.AxisListType

    N, C = x.shape
    E = dst.shape[0]
    HID = ffn_W1.shape[1]
    NX = ffn_Wg.shape[1]
    KC = C // P
    KH = HID // P
    T = 4
    GE = T * P
    W = 96
    SLOTS = 8
    HALF = SLOTS // 2
    ITERS = -(-E // (GE * SLOTS))
    NG = ITERS * SLOTS
    NH = NG // HALF
    NB = -(-N // P)
    LAST = N - (NB - 1) * P
    NPAD = NB * P
    DEPTH = 5
    AGG = NPAD + W
    GCH = -(-NG // P)
    TBL = NG + 8
    FULL_ROWS = E // GE
    LAST_EDGES = E - FULL_ROWS * GE
    BODY = (GCH - 1) * P
    TAILG = NG - BODY
    NT = NB + NX - 1
    REG = NPAD + NX * P
    QB = 4
    PAY = HID + C
    FAR = float(1 << 22)
    EPS = 1e-5
    PACK = 14
    KWIN = (N - 1) // W
    LNC = NB // T
    LNI = LNC // SLOTS
    LTAIL = NB - LNC * T
    assert SLOTS == 2 * HALF and HALF == 4 and NB < 256 and NPAD < (1 << PACK)
    assert NX * REG < (1 << 22) and NT * P <= REG and 0 < TAILG <= 32 and FULL_ROWS > BODY
    assert LNC == LNI * SLOTS and LTAIL == 2 and NT % QB == 1 and NB % 2 == 0 and NH < P

    xn_d = nc.dram_tensor("xn_scratch", [N, C], f32, kind="Internal").ap()
    h1_d = nc.dram_tensor("h1_scratch", [NPAD, C], f32, kind="Internal").ap()
    pay_d = nc.dram_tensor("pay_scratch", [NPAD, PAY], f32, kind="Internal").ap()
    list_d = nc.dram_tensor("list_scratch", [NX * REG, 2], i32, kind="Internal").ap()
    gtab_d = nc.dram_tensor("group_scratch", [2, GCH * P], i32, kind="Internal").ap()

    ctx = ExitStack()
    with ctx:
        def sb(name, shape, dt=f32):
            return ctx.enter_context(nc.sbuf_tensor(name, shape, dt))

        def ps(name, shape):
            return ctx.enter_context(nc.psum_tensor(name, shape, f32))

        def sem(name):
            return ctx.enter_context(nc.semaphore(name))

        aggT = sb("aggT", [P, KC, AGG])
        rows = sb("rows", [P, SLOTS, T, C])
        tdst = sb("tdst", [P, T, TBL])
        twgt = sb("twgt", [P, T, TBL])
        tsrc = sb("tsrc", [P, T, TBL])
        idx = sb("idx", [P, 2, HALF, T], i32)
        S = sb("S", [P, 2, T, W])
        Sov = sb("Sov", [P, T, W])
        cur = sb("cur", [P, T])
        woff = sb("woff", [P, KWIN + 1])
        regs = sb("regs", [1, NH, 4], i32)
        wins = sb("wins", [1, NG, 2], i32)
        wg1 = sb("wg1", [P, KC, C])
        wg2 = sb("wg2", [P, KC, C])
        w1 = sb("w1", [P, KC, HID])
        wgate = sb("wgate", [P, KH, NX])
        b1col = sb("b1col", [P, KH])
        brow = sb("brow", [1, 2 * C + NX])
        ident = sb("ident", [P, P])
        ones = sb("ones", [P, P])
        before = sb("before", [P, P])
        iota_w = sb("iota_w", [P, W])
        stats = sb("stats", [P, 2, T, 6])
        mv = sb("mv", [P, 2, T, 2])
        std = sb("std", [P, 2, T])
        rstd = sb("rstd", [P, 2, T])
        nmr = sb("nmr", [P, 2, T])
        zeros = sb("zeros", [P, KC, P])
        stage = sb("stage", [P, KC, P])
        zneg = sb("zneg", [P, C])
        zexp = sb("zexp", [P, C])
        work = sb("work", [P, 16 * C])
        HT = work[:, 0:HID].rearrange("p (k n) -> p k n", k=KH)
        hid = work[:, HID:2 * HID].rearrange("p (k n) -> p k n", k=KH)
        payh = work[:, 2 * HID:3 * HID]
        w0 = 3 * HID
        xnT = work[:, w0:w0 + C].rearrange("p (k n) -> p k n", k=KC)
        xn2, x1, xb = (work[:, w0 + C * n:w0 + C * (n + 1)] for n in (1, 2, 3))
        helu, hout = payh[:, 0:C], payh[:, C:2 * C]
        eneg = sb("eneg", [P, C])
        esum = sb("esum", [P, C])
        bstat = sb("bstat", [P, 6])
        bmv = sb("bmv", [P, 2])
        bstd = sb("bstd", [P, 2])
        LG = sb("LG", [P, NB + DEPTH, NX])
        epsc = sb("epsc", [P, 1])
        prefer = sb("prefer", [P, NX])
        first = sb("first", [P, NX])
        tnum = sb("tnum", [1, NT])
        node = sb("node", [P, NB])
        fill = sb("fill", [P, REG // P, 2], i32)
        pstage = sb("pstage", [P, 2], i32)
        nstage = sb("nstage", [P, 2, 2], i32)
        ids = sb("ids", [P, QB, 2], i32)
        etab = sb("etab", [1, 2, NT], i32)
        flat = aggT[:, :, :].rearrange("p k n -> p (k n)")
        RW = GCH * GE

        def table(n, dt=f32):
            v = flat[:, n * RW:(n + 1) * RW]
            return (v if dt is f32 else v.bitcast(dt)).rearrange("p (c e) -> p c e", c=GCH)

        rdst_i, rsrc_i, rwgt, rdst, rsrc, rrel = table(0, i32), table(1, i32), table(2), table(3), table(4), table(5)

        def gvec(n, dt=f32):
            v = flat[:, 6 * RW + n * GCH:6 * RW + (n + 1) * GCH]
            return v if dt is f32 else v.bitcast(dt)

        def grow(n, dt=f32):
            v = work[0:1, n * GCH * P:(n + 1) * GCH * P]
            return v if dt is f32 else v.bitcast(dt)

        rflat = rows[:, :, :, :].rearrange("p s t c -> p (s t c)")

        def gate(n):
            return rflat[:, n * NB * NX:(n + 1) * NB * NX].rearrange("p (b e) -> p b e", e=NX)

        def per_node(n):
            return rflat[:, 7 * NB * NX + n * NB:7 * NB * NX + (n + 1) * NB]

        wdk = flat[:, 0:NX * KH * C].rearrange("p (k xc) -> p k xc", k=KH)
        o1 = NX * KH * C
        bd = flat[0:1, o1:o1 + NX * C]
        o2 = o1 + NX * C
        obuf = flat[:, o2:o2 + QB * C].rearrange("p (b c) -> p b c", b=QB)
        payx = flat[:, o2 + QB * C:o2 + QB * C + QB * PAY].rearrange("p (b f) -> p b f", b=QB)
        HTx = work[:, 0:2 * HID].rearrange("p (b k n) -> p b k n", b=2, k=KH)
        assert o2 + QB * C + QB * PAY <= KC * AGG and 6 * RW + 8 * GCH <= KC * AGG
        assert 8 * GCH * P <= 16 * C and 7 * NB * NX + 12 * NB <= SLOTS * T * C

        pA = ps("pA", [P, 2, 512])
        pZ = ps("pZ", [P, 512])
        pT = ps("pT", [P, 512])
        pB = ps("pB", [P, 1024])
        pC = ps("pC", [P, 1024])
        pOV = pZ[:, C:C + KC * W]
        pLG = pA[:, 1, KC * W:KC * W + NX]

        block = ctx.enter_context(nc.Block())

        s_held = {e.engine: sem(f"held_{n}") for n, e in
                  (("sync", nc.sync), ("pool", nc.gpsimd), ("dve", nc.vector), ("act", nc.scalar))}
        s_const = sem("constants_ready")
        NCONST = 12
        s_rows_clear = sem("edge_rows_padded")
        s_rows = sem("edge_rows_loaded")
        s_w = sem("weights_loaded")
        s_tchain = sem("dve_table_step")
        s_float = sem("edge_rows_float")
        s_tT = sem("table_transposed")
        s_tcopied = sem("table_copied")
        s_gvec = sem("group_vectors_ready")
        s_gst = sem("group_vectors_stored")
        s_gld = sem("group_rows_loaded")
        s_regs = sem("register_table_ready")
        s_tbl_clear = sem("tables_cleared")
        s_xin = [sem(f"x_loaded_{i}") for i in range(SLOTS)]
        s_xst = [sem(f"xn_stored_{i}") for i in range(SLOTS)]
        s_ln = sem("dve_layernorm_step")
        s_var = sem("variance_ready")
        s_std = sem("std_ready")
        s_nmr = sem("layernorm_scales_ready")
        s_nd = sem("normalised_by_dve")
        s_na = sem("normalised_by_act")
        s_np = sem("normalised_by_pool")
        s_aggclear = sem("aggT_cleared")
        s_blkclear = sem("aggT_block_cleared")
        s_idx = [sem(f"indices_staged_{l}") for l in range(2)]
        s_gath = [[sem(f"rows_gathered_{l}_{i}") for i in range(SLOTS)] for l in range(2)]
        s_S = [sem(f"S_ready_{l}") for l in range(2)]
        s_mm = [sem(f"group_multiplied_{l}") for l in range(2)]
        s_add = [sem(f"group_added_{l}") for l in range(2)]
        s_ovS = [sem(f"overflow_S_ready_{l}") for l in range(2)]
        s_ovmm = [sem(f"overflow_multiplied_{l}") for l in range(2)]
        s_ovadd = [sem(f"overflow_added_{l}") for l in range(2)]
        s_ovc = [sem(f"overflow_window_moved_{l}") for l in range(2)]
        s_stage = [sem(f"block_staged_{l}") for l in range(2)]
        s_z = [sem(f"Z_ready_{l}") for l in range(2)]
        s_zexp = [sem(f"Z_exp_ready_{l}") for l in range(2)]
        s_zneg = [sem(f"Z_negative_part_{l}") for l in range(2)]
        s_elu = [sem(f"elu_ready_{l}") for l in range(2)]
        s_free = [sem(f"elu_store_done_{l}") for l in range(2)]
        s_eln = [sem(f"elu_step_{l}") for l in range(2)]
        s_zused = sem("Z_used_2")
        s_h1st = sem("h1_stored")
        s_x1st = sem("x1_stored")
        s_xb = sem("x_block_loaded")
        s_tick = sem("dve_tick_step")
        s_var2 = sem("block_variance_ready")
        s_std2 = sem("block_std_ready")
        s_xn2 = sem("block_normalised")
        s_xT = sem("block_transposed")
        s_xTc = sem("block_transpose_copied")
        s_hT = sem("hidden_ready")
        s_hb = sem("hidden_biased")
        s_gelu = sem("hidden_activated")
        s_log = sem("logits_ready")
        s_lg = sem("logits_copied")
        s_hback = sem("hidden_transposed_back")
        s_payc = sem("hidden_rows_copied")
        s_payst = sem("hidden_rows_stored")
        s_payfree = sem("hidden_rows_store_done")
        s_fill = sem("lists_filled")
        s_gate = sem("dve_gate_step")
        s_dlog = sem("logits_less_max_ready")
        s_gexp = sem("gate_exp_ready")
        s_oh = sem("choice_ready")
        s_rank = sem("ranks_ready")
        s_place = sem("places_staged")
        s_list = [sem(f"list_scattered_{i}") for i in range(2)]
        s_wd = sem("expert_weights_loaded")
        s_et = sem("dve_expert_table_step")
        s_etr = sem("expert_table_ready")
        s_ids = [sem(f"ids_loaded_{i}") for i in range(QB)]
        s_pg = [sem(f"payload_gathered_{i}") for i in range(QB)]
        s_eT = sem("expert_tile_transposed")
        s_eTa = sem("expert_tile_copied_by_act")
        s_eTd = sem("expert_tile_copied_by_dve")
        s_y = sem("expert_output_ready")
        s_o = sem("output_tile_ready")
        s_out = [sem(f"output_scattered_{i}") for i in range(QB)]

        def need(eng, semaphore, value):
            if isinstance(value, int) and value < 1:
                return
            eng.wait_ge(semaphore, value)

        def hold(eng, semaphore, value):
            if isinstance(value, int) and value < 1:
                return
            eng.wait_ge(semaphore, value)
            if not isinstance(value, int):
                eng.sem_inc(s_held[eng.engine], 1)

        class Steps:

            def __init__(self, eng, semaphore):
                self.eng, self.sem, self.base, self.n = eng, semaphore, 0, 0

            def then(self, ins, own=False):
                self.n += 1
                ins.then_inc(self.sem, 1)
                (hold if own else need)(self.eng, self.sem, self.base + self.n)

        def within(value, low, high):
            return nc.s_assert_within(value, low, high, skip_runtime_bounds_check_because=
                                      "windows end at the group's largest dst, which is below the number of nodes")

        def runs(eng, count):
            yield 0
            with eng.Fori(1, count - 1) as i:
                yield i
            yield count - 1

        def flows(k, j):
            return not isinstance(j, int) or j - k < NB

        def half_flags(eng, h):
            v = eng.value_load(regs[0:1, bass.ds(h, 1), 0], min_val=0, max_val=(1 << 17) - 1)
            return v >> 16, (v >> 8) & 255, v & 255

        def overflow_windows(eng, g):
            ws = eng.value_load(wins[0:1, bass.ds(g, 1), 0], min_val=0, max_val=NG * P)
            we = eng.value_load(wins[0:1, bass.ds(g, 1), 1], min_val=0, max_val=NG * P)
            return ws, we

        def ticks(eng, start, end, tick):
            with eng.If(start < end):
                with eng.Fori(start, end) as j:
                    tick(nc.s_assert_within(j, 0, NB - 1, skip_runtime_bounds_check_because=
                                            "the table's last end is the number of blocks"))

        @block.sync
        def _(sp):
            def x_chunk(c):
                return x[bass.ds(c * (T * P), T * P), :].rearrange("(t p) f -> p t f", p=P)

            def xn_chunk(c):
                return xn_d[bass.ds(c * (T * P), T * P), :].rearrange("(t p) f -> p t f", p=P)

            AHEAD = SLOTS - 2
            for c in range(2):
                sp.dma_start(rows[:, c, :, :], x_chunk(c)).then_inc(s_xin[c], 16)
            sp.wait_ge(s_rows_clear, 3)
            for to, frm in ((rdst_i, dst), (rsrc_i, src), (rwgt, edge_weight)):
                sp.dma_start(to[:, 0:GCH - 1, :],
                             frm[0:BODY * GE].rearrange("(c p e) -> p c e", p=P, e=GE)).then_inc(s_rows, 16)
                sp.dma_start(to[0:FULL_ROWS - BODY, GCH - 1, :],
                             frm[BODY * GE:FULL_ROWS * GE].rearrange("(p e) -> p e", e=GE)).then_inc(s_rows, 16)
                sp.dma_start(to[FULL_ROWS - BODY:FULL_ROWS - BODY + 1, GCH - 1, 0:LAST_EDGES],
                             frm[FULL_ROWS * GE:E].rearrange("(a e) -> a e", a=1)).then_inc(s_rows, 16)
            for c in range(2, AHEAD):
                sp.dma_start(rows[:, c, :, :], x_chunk(c)).then_inc(s_xin[c], 16)
            for i in runs(sp, LNI):
                for s in range(SLOTS):
                    c = SLOTS * i + s
                    to = (s + AHEAD) % SLOTS
                    if not isinstance(i, int) or c + AHEAD <= LNC:
                        need(sp, s_xst[to], 16 * (i + 1 if s >= 2 else i))
                        if isinstance(i, int) and c + AHEAD == LNC:
                            sp.dma_start(rows[:, to, 0, :], x[LNC * T * P:(NB - 1) * P, :]).then_inc(s_xin[to], 16)
                            sp.dma_start(rows[0:LAST, to, 1, :], x[(NB - 1) * P:N, :]).then_inc(s_xin[to], 16)
                        else:
                            sp.dma_start(rows[:, to, :, :], x_chunk(c + AHEAD)).then_inc(s_xin[to], 16)
                    sp.wait_ge(s_nd, c + 1)
                    sp.wait_ge(s_na, c + 1)
                    sp.wait_ge(s_np, c + 1)
                    sp.dma_start(xn_chunk(c), rows[:, s, :, :]).then_inc(s_xst[s], 16)
            sp.wait_ge(s_nd, LNC + 1)
            sp.wait_ge(s_na, LNC + 1)
            sp.dma_start(xn_d[LNC * T * P:(NB - 1) * P, :], rows[:, 0, 0, :]).then_inc(s_xst[0], 16)
            sp.dma_start(xn_d[(NB - 1) * P:N, :], rows[0:LAST, 0, 1, :]).then_inc(s_xst[0], 16)

            for to, frm in ((wg1, gnn_W1), (wg2, gnn_W2), (w1, ffn_W1), (wgate, ffn_Wg)):
                sp.dma_start(to[:, :, :], frm.rearrange("(k p) n -> p k n", p=P)).then_inc(s_w, 16)
            for at, frm in ((0, gnn_b1), (C, gnn_b2), (2 * C, ffn_bg)):
                sp.dma_start(brow[0:1, at:at + frm.shape[0]], frm.rearrange("(a n) -> a n", a=1)).then_inc(s_w, 16)
            with nc.allow_non_contiguous_dma(reason="1024 bias values, once"):
                sp.dma_start(b1col[:, :], ffn_b1.rearrange("(k p) -> p k", p=P)).then_inc(s_w, 16)

            sp.wait_ge(s_const, NCONST)
            for e in range(NX):
                sp.dma_start(list_d[e * REG:(e + 1) * REG, :].rearrange("(p n) a -> p n a", p=P), fill[:, :, :])\
                  .then_inc(s_fill, 16)

            sp.sem_inc(s_free[0], 1)
            sp.wait_ge(s_elu[0], 2)
            sp.sem_inc(s_free[0], 1)
            with sp.Fori(0, NB) as b:
                sp.wait_ge(s_elu[0], b + 3)
                sp.dma_start(h1_d[bass.ds(b * P, P), :], hout).then_inc(s_h1st, 16)
                sp.wait_ge(s_h1st, 16 * (b + 1))
                sp.sem_inc(s_free[0], 1)

            sp.sem_inc(s_free[1], 1)
            sp.sem_inc(s_payfree, 1)
            sp.wait_ge(s_elu[1], 1)
            sp.dma_start(xb, x[0:P, :]).then_inc(s_xb, 16)

            def blocks_io(j, load=None, x1_rows=True, hidden_rows=True):
                if x1_rows or load is not None:
                    sp.wait_ge(s_elu[1], j + 2)
                if load is not None:
                    load()
                if x1_rows:
                    sp.dma_start(pay_d[bass.ds((j - 1) * P, P), HID:PAY], x1).then_inc(s_x1st, 16)
                    sp.wait_ge(s_x1st, 16 * j)
                sp.sem_inc(s_free[1], 1)
                sp.wait_ge(s_payc, j + 2)
                if hidden_rows:
                    b = j - DEPTH
                    sp.dma_start(pay_d[bass.ds(b * P, P), 0:HID], payh).then_inc(s_payst, 16)
                    sp.wait_ge(s_payst, 16 * (b + 1))
                sp.sem_inc(s_payfree, 1)

            def load_x(j):
                sp.dma_start(xb, x[bass.ds(j * P, P), :]).then_inc(s_xb, 16)

            for j in range(DEPTH):
                blocks_io(j, lambda: load_x(j), x1_rows=j > 0, hidden_rows=False)
            with sp.Fori(DEPTH, NB - 1) as j:
                blocks_io(j, lambda: load_x(j))
            blocks_io(NB - 1, lambda: sp.dma_start(xb[0:LAST, :], x[(NB - 1) * P:N, :]).then_inc(s_xb, 16))
            for j in range(NB, NB + DEPTH):
                blocks_io(j, x1_rows=j == NB)

            sp.wait_ge(s_stage[1], NB + 1)
            for k in range(KH):
                sp.dma_start(wdk[:, k, :].rearrange("p (x c) -> p x c", x=NX),
                             ffn_Wd[:, k * P:(k + 1) * P, :].rearrange("x p c -> p x c")).then_inc(s_wd, 16)
            sp.dma_start(bd, ffn_bd.rearrange("x (a c) -> a (x c)", a=1)).then_inc(s_wd, 16)

            def load_ids(t, q):
                at = sp.value_load(etab[0:1, 1, bass.ds(t, 1)], min_val=0, max_val=NX * REG - P)
                sp.dma_start(ids[:, q, :], list_d[bass.ds(at, P), :]).then_inc(s_ids[q], 16)

            for b2 in range(2):
                sp.wait_ge(s_list[b2], 16 * (NB // 2))
            sp.wait_ge(s_etr, 1)
            for q in range(QB):
                load_ids(q, q)
            with sp.Fori(0, NT // QB - 1) as i:
                for q in range(QB):
                    sp.wait_ge(s_out[q], 16 * (i + 1))
                    load_ids(QB * i + QB + q, q)
            sp.wait_ge(s_out[0], 16 * (NT // QB))
            load_ids(NT - 1, 0)
            sp.wait_ge(s_out[0], 16 * (NT // QB + 1))
            for q in range(1, QB):
                sp.wait_ge(s_out[q], 16 * (NT // QB))

        @block.gpsimd
        def _(pool):
            pool.memset(rdst_i[0:TAILG, GCH - 1, :], N - 1).then_inc(s_rows_clear, 1)
            pool.memset(rsrc_i[0:TAILG, GCH - 1, :], 0).then_inc(s_rows_clear, 1)
            pool.memset(rwgt[0:TAILG, GCH - 1, :], 0.0).then_inc(s_rows_clear, 1)
            pool.memset(ones[:, :], 1.0).then_inc(s_const, 1)
            pool.wait_ge(s_const, 1)
            pool.affine_select(out=ident[:, :], in_=ones[:, :], compare_op=ALU.is_equal, fill=0.0, base=0,
                               pattern=[[-1, P]], channel_multiplier=1).then_inc(s_const, 1)
            pool.affine_select(out=before[:, :], in_=ones[:, :], compare_op=ALU.is_gt, fill=0.0, base=0,
                               pattern=[[1, P]], channel_multiplier=-1).then_inc(s_const, 1)
            for t in (tdst, twgt, tsrc):
                pool.memset(t[:, :, NG:TBL], 0.0).then_inc(s_tbl_clear, 1)
            for to, pattern, base, per_lane in ((iota_w, [[1, W]], 0, 0), (woff, [[W, KWIN + 1]], 0, 0),
                                                (prefer, [[-1, NX]], NX, 0), (first, [[REG, NX]], 0, 0),
                                                (tnum, [[1, NT]], 0, 0), (node, [[P, NB]], 0, 1)):
                pool.iota(to[:, :], pattern, base=base, channel_multiplier=per_lane,
                          allow_small_or_imprecise_dtypes=True).then_inc(s_const, 1)
            pool.memset(fill[:, :, 0], N).then_inc(s_const, 1)
            pool.memset(fill[:, :, 1], 0).then_inc(s_const, 1)
            pool.memset(zeros[:, :, :], 0.0).then_inc(s_const, 1)

            pool.wait_ge(s_gvec, 1)
            with nc.allow_non_contiguous_dma(reason="512 values each, once"):
                pool.dma_start(gtab_d[0, :].rearrange("(c p) -> p c", p=P), gvec(7, i32)).then_inc(s_gst, 16)
                pool.dma_start(gtab_d[1, :].rearrange("(c p) -> p c", p=P), gvec(4, i32)).then_inc(s_gst, 16)
            pool.wait_ge(s_gst, 32)
            pool.dma_start(grow(0, i32), gtab_d[0:1, :]).then_inc(s_gld, 16)
            pool.dma_start(grow(1, i32), gtab_d[1:2, :]).then_inc(s_gld, 16)

            for i in runs(pool, LNI):
                for s in range(SLOTS):
                    c = SLOTS * i + s
                    hold(pool, s_nmr, c + 1)
                    pool.tensor_scalar(rows[:, s, T - 1, :], rows[:, s, T - 1, :], mv[:, s % 2, T - 1, 0:1],
                                       rstd[:, s % 2, T - 1:T], ALU.subtract, ALU.mult).then_inc(s_np, 1)
                if isinstance(i, int) and i == 0:
                    pool.wait_ge(s_tcopied, 3 * GCH)
                    pool.memset(aggT[:, 0, :], 0.0).then_inc(s_aggclear, 1)
                if isinstance(i, int) and i == LNI - 1:
                    pool.memset(aggT[:, 1, :], 0.0).then_inc(s_aggclear, 1)

            for layer, source in ((0, xn_d), (1, h1_d)):
                if layer == 0:
                    pool.wait_ge(s_xst[0], 16 * (LNI + 2))
                    for s in range(1, SLOTS):
                        pool.wait_ge(s_xst[s], 16 * LNI)
                else:
                    pool.wait_ge(s_h1st, 16 * NB)
                with pool.Fori(0, ITERS) as i:
                    for s in range(SLOTS):
                        g = SLOTS * i + s
                        if s % HALF == 0:
                            hold(pool, s_idx[layer], 2 * i + s // HALF + 1)
                        hold(pool, s_mm[layer], g + 1)
                        for t in range(T):
                            at = idx[:, s // HALF, s % HALF, t:t + 1]
                            pool.indirect_dma_start(rows[:, s, t, :], None, source,
                                                    bass.IndirectOffsetOnAxis(at, 0))\
                                .then_inc(s_gath[layer][s], 16)

            pool.wait_ge(s_fill, 16 * NX)
            with pool.Fori(0, NB // 2) as i:
                for b2 in range(2):
                    hold(pool, s_place, 2 * i + b2 + 1)
                    pool.indirect_dma_start(list_d, bass.IndirectOffsetOnAxis(pstage[:, b2:b2 + 1], 0),
                                            nstage[:, b2, :], None,
                                            bounds_check=NX * REG - 1, oob_is_err=False).then_inc(s_list[b2], 16)

            pool.wait_ge(s_payst, 16 * NB)
            pool.wait_ge(s_x1st, 16 * NB)
            pool.wait_ge(s_stage[1], NB + 1)

            def gather(i, q):
                hold(pool, s_ids[q], 16 * (i + 1))
                pool.indirect_dma_start(payx[:, q, :], None, pay_d,
                                        bass.IndirectOffsetOnAxis(ids[:, q, 0:1], 0)).then_inc(s_pg[q], 16)

            def scatter(t, q):
                hold(pool, s_o, t + 3)
                pool.indirect_dma_start(out, bass.IndirectOffsetOnAxis(ids[:, q, 0:1], 0), obuf[:, q, :],
                                        None, bounds_check=N - 1, oob_is_err=False).then_inc(s_out[q], 16)

            LEAD = QB - 1
            for q in range(LEAD):
                gather(0, q)
            with pool.Fori(0, NT // QB - 1) as i:
                for q in range(QB):
                    scatter(QB * i + q, q)
                    gather(i + (q + LEAD) // QB, (q + LEAD) % QB)
            for t in range(NT - 1 - QB, NT):
                scatter(t, t % QB)
                if t + LEAD < NT:
                    gather((t + LEAD) // QB, (t + LEAD) % QB)

        @block.scalar
        def _(act):
            for n in range(3 * GCH):
                c = n % GCH
                cnt = P if c < GCH - 1 else TAILG
                act.wait_ge(s_tT, n + 1)
                act.activation((tdst, tsrc, twgt)[n // GCH][:, :, c * P:c * P + cnt],
                               pB[:, (n % 2) * 512:(n % 2 + 1) * 512].rearrange("p (t g) -> p t g", t=T)[:, :, 0:cnt],
                               ACT.Copy).then_inc(s_tcopied, 1)

            def root(c, par, n):
                act.wait_ge(s_var, c + 1)
                act.activation(std[:, par, 0:n], mv[:, par, 0:n, 1], ACT.Sqrt, bias=epsc[:, :]).then_inc(s_std, 1)

            def normalise(c, slot, par, n):
                act.wait_ge(s_nmr, c + 1)
                for t in range(1, max(n - 1, 2)):
                    last = act.activation(rows[:, slot, t, :], rows[:, slot, t, :], ACT.Identity,
                                          bias=nmr[:, par, t:t + 1], scale=rstd[:, par, t:t + 1])
                last.then_inc(s_na, 1)

            for i in runs(act, LNI):
                for s in range(SLOTS):
                    c = SLOTS * i + s
                    root(c, s % 2, T)
                    if not (isinstance(c, int) and c == 0):
                        normalise(c - 1, (s - 1) % SLOTS, (s - 1) % 2, T)
            root(LNC, 0, LTAIL)
            normalise(LNC - 1, SLOTS - 1, 1, T)
            normalise(LNC, 0, 0, LTAIL)

            act.wait_ge(s_tcopied, 3 * GCH)
            act.wait_ge(s_regs, 1)
            act.wait_ge(s_const, NCONST)

            def stage_block(layer, j, h):
                act.wait_ge(s_add[layer], HALF * (h + 1) + 2)
                hold(act, s_z[layer], j + 1)
                act.activation(stage[:, :, :], aggT[:, :, bass.ds(j * P, P)], ACT.Copy).then_inc(s_stage[layer], 1)

            def exponent(layer, j):
                act.wait_ge(s_z[layer], j + 1)
                act.wait_ge(s_elu[layer], j + 1)
                act.activation(zneg[:, :], pZ[:, 0:C], ACT.Relu, scale=-1.0).then_inc(s_zneg[layer], 1)
                act.wait_ge(s_zneg[layer], j + 1)
                act.activation(zexp[:, :], zneg[:, :], ACT.Exp, scale=-1.0).then_inc(s_zexp[layer], 1)

            def tick1(j, h):
                if flows(0, j):
                    stage_block(0, j, h)
                exponent(0, j)
                if flows(0, j):
                    hold(act, s_stage[0], j + 2)
                    act.activation(aggT[:, :, bass.ds(j * P, P)], zeros[:, :, :], ACT.Copy).then_inc(s_blkclear, 1)

            def tick2(j, h):
                if flows(0, j):
                    stage_block(1, j, h)
                if flows(1, j):
                    exponent(1, j)
                if flows(2, j):
                    act.wait_ge(s_var2, j + 1)
                    act.wait_ge(s_xn2, j + 1)
                    act.activation(bstd[:, 0:1], bmv[:, 1:2], ACT.Sqrt, bias=epsc[:, :]).then_inc(s_std2, 1)
                act.wait_ge(s_hback, j + 2)
                act.wait_ge(s_payfree, j + 1)
                act.activation(payh, pC[:, :], ACT.Copy).then_inc(s_payc, 1)
                if flows(4, j):
                    act.wait_ge(s_hb, j + 2)
                    act.wait_ge(s_log, j + 2)
                    act.activation(HT, hid, ACT.Gelu).then_inc(s_gelu, 1)

            for sm in (s_stage[0], s_zexp[0], s_stage[1], s_zexp[1], s_std2, s_gelu, s_payc):
                act.sem_inc(sm, 1)
            for layer in range(2):
                with act.Fori(0, ITERS) as i:
                    for half in range(2):
                        h = 2 * i + half
                        _, start, end = half_flags(act, h)
                        ticks(act, start, end, lambda j: (tick1, tick2)[layer](j, h))
                if layer == 0:
                    tick1(NB, None)
            for j in range(NB, NB + DEPTH):
                tick2(j, None)

            act.wait_ge(s_dlog, 1)
            act.activation(gate(1), gate(0), ACT.Exp).then_inc(s_gexp, 1)

            def copy_half(t, b2):
                act.wait_ge(s_eT, t + 1)
                act.wait_ge(s_y, t + 1)
                act.activation(HTx[:, b2, 0:KH // 2, :],
                               (pB, pC)[b2][:, 0:512].rearrange("p (k n) -> p k n", k=KH // 2),
                               ACT.Copy).then_inc(s_eTa, 1)

            with act.Fori(0, NT // 2) as i:
                for b2 in range(2):
                    copy_half(2 * i + b2, b2)
            copy_half(NT - 1, 0)

        @block.vector
        def _(dve):
            v = nc.vector
            tc = Steps(dve, s_tchain)
            tc.then(v.memset(epsc[:, :], EPS))

            dve.wait_ge(s_rows, 9 * 16)
            parts = ((P, slice(0, GCH - 1)), (TAILG, slice(GCH - 1, GCH)))
            for n, c in parts:
                v.tensor_copy(rsrc[0:n, c, :], rsrc_i[0:n, c, :]).then_inc(s_float, 1)
                tc.then(v.tensor_copy(rdst[0:n, c, :], rdst_i[0:n, c, :]))
            LO, HI, D, Q = gvec(0), gvec(1), gvec(2), gvec(3)
            LOi, Di, Qi, NVi = gvec(4, i32), gvec(5, i32), gvec(6, i32), gvec(7, i32)
            tc.then(v.memset(flat[:, 6 * RW:6 * RW + 2 * GCH], 0.0))
            for n, c in parts:
                v.tensor_reduce(LO[0:n, c], rdst[0:n, c, :], axis=AX.X, op=ALU.min)
                tc.then(v.tensor_reduce(HI[0:n, c], rdst[0:n, c, :], axis=AX.X, op=ALU.max))
            for c in range(GCH):
                n = P if c < GCH - 1 else TAILG
                v.tensor_scalar(rrel[0:n, c, :], rdst[0:n, c, :], LO[0:n, c:c + 1], None, ALU.subtract)\
                 .then_inc(s_float, 1)
            assert W == 96
            tc.then(v.tensor_tensor(D, HI, LO, ALU.subtract))
            tc.then(v.tensor_copy(Di, D))
            tc.then(v.tensor_scalar(Qi, Di, 5, None, ALU.arith_shift_right))
            tc.then(v.tensor_copy(Q, Qi))
            tc.then(v.tensor_scalar(D, Q, 21846.0, None, ALU.mult))
            tc.then(v.tensor_copy(Di, D))
            tc.then(v.tensor_scalar(NVi, Di, 16, None, ALU.arith_shift_right))
            v.tensor_copy(LOi, LO).then_inc(s_gvec, 1)

            lnc = Steps(dve, s_ln)

            def statistics(c, slot, par, n):
                for t in range(n):
                    last = v.bn_stats(stats[:, par, t, :], rows[:, slot, t, :])
                lnc.then(last, own=True)
                for t in range(n):
                    last = v.bn_aggr(mv[:, par, t, :], stats[:, par, t, :])
                last.then_inc(s_var, 1)

            def scales(c, slot, par, n):
                dve.wait_ge(s_std, c + 1)
                lnc.then(v.reciprocal(rstd[:, par, 0:n], std[:, par, 0:n]))
                v.scalar_tensor_tensor(out=nmr[:, par, 0:n], in0=mv[:, par, 0:n, 0], scalar=-1.0,
                                       in1=rstd[:, par, 0:n], op0=ALU.mult, op1=ALU.mult).then_inc(s_nmr, 1)
                v.tensor_scalar(rows[:, slot, 0, :], rows[:, slot, 0, :], mv[:, par, 0, 0:1], rstd[:, par, 0:1],
                                ALU.subtract, ALU.mult).then_inc(s_nd, 1)

            for i in runs(dve, LNI):
                first_chunk = isinstance(i, int) and i == 0
                lnc.base, lnc.n = 0 if first_chunk else 2 * SLOTS * i - 1, 0
                for s in range(SLOTS):
                    c = SLOTS * i + s
                    dve.wait_ge(s_xin[s], 16 * (i + 1))
                    need(dve, s_na, c - 1)
                    need(dve, s_np, c - 1)
                    statistics(c, s, s % 2, T)
                    if s or not first_chunk:
                        scales(c - 1, (s - 1) % SLOTS, (s - 1) % 2, T)
            lnc.base, lnc.n = 2 * LNC - 1, 0
            dve.wait_ge(s_xin[0], 16 * (LNI + 2))
            dve.wait_ge(s_na, LNC - 1)
            dve.wait_ge(s_np, LNC - 1)
            statistics(LNC, 0, 0, LTAIL)
            scales(LNC - 1, SLOTS - 1, 1, T)
            scales(LNC, 0, 0, LTAIL)

            dve.wait_ge(s_gld, 32)
            NVr, LOr, NVf, INC, STA = grow(0, i32), grow(1, i32), grow(2), grow(3), grow(4)
            tc.then(v.tensor_copy(NVf, NVr))
            tc.then(v.tensor_tensor_scan(INC, NVf, NVf, 0.0, ALU.add, ALU.bypass))
            tc.then(v.tensor_tensor(STA, INC, NVf, ALU.subtract))
            for r, frm in ((0, STA), (1, INC)):
                tc.then(v.tensor_copy(wins[0:1, :, r], frm[:, 0:NG]))
            LO4 = LOr[:, 0:NG].rearrange("o (h g) -> o h g", g=HALF)
            for r in range(2):
                pair = regs[0:1, :, 1 + r]
                tc.then(v.tensor_scalar(pair, LO4[:, :, 2 * r + 1], PACK, None, ALU.logical_shift_left))
                tc.then(v.tensor_tensor(pair, pair, LO4[:, :, 2 * r], ALU.bitwise_or))
            LOf, A, B, R = grow(2), grow(5), grow(6), grow(7, i32)
            FL = LOf[:, 0:NH]
            tc.then(v.tensor_copy(LOf, LOr))
            tc.then(v.memset(work[0:1, 5 * GCH * P:7 * GCH * P], float(NPAD)))
            tc.then(v.tensor_reduce(A[:, 0:NH], LOf[:, 0:NG].rearrange("o (h g) -> o h g", g=HALF),
                                    axis=AX.X, op=ALU.min))
            d = 1
            while d <= NH:
                tc.then(v.tensor_tensor(B[:, 0:NH + 1], A[:, 0:NH + 1], A[:, d:d + NH + 1], ALU.min))
                A, B, d = B, A, 2 * d
            tc.then(v.tensor_copy(R[:, 0:NH], A[:, 1:NH + 1]))
            tc.then(v.tensor_scalar(R[:, 0:NH], R[:, 0:NH], 7, None, ALU.arith_shift_right))
            tc.then(v.tensor_copy(A[:, 0:NH], R[:, 0:NH]))
            INC4, STA4 = (a[:, 0:NG].rearrange("o (h g) -> o h g", g=HALF) for a in (INC, STA))
            tc.then(v.tensor_tensor(FL, INC4[:, :, HALF - 1], STA4[:, :, 0], ALU.subtract))
            tc.then(v.tensor_scalar(FL, FL, 1.0, 65536.0, ALU.min, ALU.mult))
            tc.then(v.tensor_tensor(FL, FL, A[:, 0:NH], ALU.add))
            tc.then(v.scalar_tensor_tensor(out=FL[:, 1:NH], in0=A[:, 0:NH - 1], scalar=256.0, in1=FL[:, 1:NH],
                                           op0=ALU.mult, op1=ALU.add))
            tc.then(v.tensor_copy(regs[0:1, :, 0], FL))
            tc.then(v.memset(work[:, :], 0.0))
            tc.then(v.memset(pZ[:, 0:C], 0.0))
            tc.then(v.memset(pT[:, 0:C], 0.0))
            v.memset(bmv[:, :], 1.0).then_inc(s_regs, 1)
            for sm in (s_zused, s_xn2, s_hb, s_elu[0], s_elu[1], s_var2, s_xTc, s_lg):
                dve.sem_inc(sm, 1)
            dve.sem_inc(s_o, 2)

            dve.wait_ge(s_const, NCONST)
            dve.wait_ge(s_tcopied, 3 * GCH)
            dve.wait_ge(s_tbl_clear, 3)
            dve.wait_ge(s_regs, 1)
            dve.wait_ge(s_aggclear, 2)

            def build_S(layer, g, half):
                dve.wait_ge(s_mm[layer], g + (SLOTS - 1))
                for t in range(T):
                    last = v.tensor_scalar(S[:, half, t, :], iota_w[:, :], tdst[:, t, bass.ds(g, 1)],
                                           twgt[:, t, bass.ds(g, 1)], ALU.is_equal, ALU.mult)
                last.then_inc(s_S[layer], 1)

            def overflow(layer, g, base):
                ws, we = overflow_windows(dve, g)
                with dve.If(ws < we):
                    with dve.Fori(ws, we) as w:
                        k = within(w - ws + 1, 1, KWIN)
                        v.tensor_scalar(cur[:, :], tdst[:, :, bass.ds(g, 1)].rearrange("p t g -> p (t g)"),
                                        woff[:, bass.ds(k, 1)], None, ALU.subtract).then_inc(s_ovc[layer], 1)
                        dve.wait_ge(s_ovc[layer], w + 1)
                        for t in range(T):
                            last = v.tensor_scalar(Sov[:, t, :], iota_w[:, :], cur[:, t:t + 1],
                                                   twgt[:, t, bass.ds(g, 1)], ALU.is_equal, ALU.mult)
                        last.then_inc(s_ovS[layer], 1)
                        dve.wait_ge(s_ovmm[layer], w + 1)
                        at = within(base + k * W, 0, N - 1)
                        far = aggT[:, :, bass.ds(at, W)]
                        v.tensor_tensor(far, far, pOV.rearrange("p (k n) -> p k n", k=KC), ALU.add)\
                         .then_inc(s_ovadd[layer], 1)
                        hold(dve, s_ovadd[layer], w + 1)

            def edges_half(layer, h, half, bases, with_overflow):
                for u in range(HALF):
                    g = HALF * h + u
                    build_S(layer, g + 1, (u + 1) % 2)
                    hold(dve, s_add[layer], g + 2)
                    if with_overflow:
                        overflow(layer, g, bases[u])
                    dve.wait_ge(s_mm[layer], g + 1 + SLOTS)
                    to = aggT[:, :, bass.ds(bases[u], W)]
                    v.tensor_tensor(to, to, pA[:, u % 2, 0:KC * W].rearrange("p (k n) -> p k n", k=KC), ALU.add)\
                     .then_inc(s_add[layer], 1)

            def stage_idx(layer, h, half):
                v.tensor_copy(idx[:, half, :, :], tsrc[:, :, bass.ds(h * HALF, HALF)].rearrange("p t g -> p g t"))\
                 .then_inc(s_idx[layer], 1)

            def elu(layer, j, to):
                dve.wait_ge(s_zexp[layer], j + 2)
                v.tensor_scalar(eneg[:, :], zexp[:, :], -1.0, None, ALU.add).then_inc(s_eln[layer], 1)
                if layer == 0:
                    dve.wait_ge(s_free[0], j + 1)
                dve.wait_ge(s_eln[layer], j + 1)
                return v.scalar_tensor_tensor(out=to, in0=pZ[:, 0:C], scalar=0.0, in1=eneg[:, :],
                                              op0=ALU.max, op1=ALU.add)

            def tick1(j):
                elu(0, j, hout).then_inc(s_elu[0], 1)

            bc = Steps(dve, s_tick)

            def tick2(j):
                bc.base, bc.n = 2 * j, 0
                if flows(3, j):
                    dve.wait_ge(s_xT, j + 1)
                    dve.wait_ge(s_hT, j + 1)
                    v.tensor_copy(xnT, pT[:, 0:C].rearrange("p (k n) -> p k n", k=KC)).then_inc(s_xTc, 1)
                if flows(4, j):
                    dve.wait_ge(s_hT, j + 1)
                    dve.wait_ge(s_gelu, j + 1)
                    v.tensor_tensor(hid, pB[:, :].rearrange("p (k n) -> p k n", k=KH),
                                    b1col[:, :].unsqueeze(2).to_broadcast([P, KH, P]), ALU.add).then_inc(s_hb, 1)
                if flows(1, j):
                    hsum = elu(1, j, esum[:, :])
                    hsum.then_inc(s_zused, 1)
                if flows(2, j):
                    dve.wait_ge(s_std2, j + 2)
                    bc.then(v.reciprocal(bstd[:, 1:2], bstd[:, 0:1]))
                    dve.wait_ge(s_xT, j + 1)
                    v.tensor_scalar(xn2, x1, bmv[:, 0:1], bstd[:, 1:2], ALU.subtract, ALU.mult).then_inc(s_xn2, 1)
                if flows(1, j):
                    dve.wait_ge(s_xb, 16 * (j + 1))
                    dve.wait_ge(s_free[1], j + 1)
                    dve.wait_ge(s_zused, j + 2)
                    dve.wait_ge(s_xn2, j + 2)
                    v.tensor_tensor(x1, esum[:, :], xb, ALU.add).then_inc(s_elu[1], 1)
                    dve.wait_ge(s_elu[1], j + 2)
                    bc.then(v.bn_stats(bstat[:, :], x1), own=True)
                    v.bn_aggr(bmv[:, :], bstat[:, :]).then_inc(s_var2, 1)
                dve.wait_ge(s_log, j + 2)
                v.tensor_copy(LG[:, bass.ds(j, 1), :].rearrange("p b e -> p (b e)"), pLG).then_inc(s_lg, 1)

            for layer in range(2):
                if layer:
                    dve.wait_ge(s_blkclear, NB)
                    dve.wait_ge(s_w, 8 * 16)
                    for s in range(SLOTS):
                        dve.wait_ge(s_gath[0][s], 16 * T * ITERS)
                dve.sem_inc(s_add[layer], 2)
                for half in range(2):
                    stage_idx(layer, half, half)
                build_S(layer, 0, 0)
                with dve.Fori(0, ITERS) as i:
                    for half in range(2):
                        h = 2 * i + half
                        ovf, start, end = half_flags(dve, h)
                        bases = []
                        for r in range(2):
                            pair = dve.value_load(regs[0:1, bass.ds(h, 1), 1 + r], min_val=0,
                                                  max_val=(1 << 2 * PACK) - 1)
                            for one in (pair & ((1 << PACK) - 1), pair >> PACK):
                                bases.append(nc.s_assert_within(one, 0, N - 1, skip_runtime_bounds_check_because=
                                                                "a dst is below the number of nodes"))
                        with dve.If(ovf > 0):
                            edges_half(layer, h, half, bases, True)
                        with dve.Else():
                            edges_half(layer, h, half, bases, False)
                        stage_idx(layer, h + 2, half)
                        ticks(dve, start, end, (tick1, tick2)[layer])
                if layer == 0:
                    tick1(NB)
            for j in range(NB, NB + DEPTH):
                tick2(j)

            gc = Steps(dve, s_gate)
            dve.wait_ge(s_lg, NB + DEPTH + 1)
            dve.wait_ge(s_mm[1], NG + SLOTS)
            lg = LG[:, DEPTH:DEPTH + NB, :]
            DL, EX, SC, OH, CNT, INC, PL = (gate(n) for n in range(7))
            MX, EM, SM, RS, GATE, SMX, VAL, AT, FARV, PLACE = (per_node(n) for n in range(10))

            def wide(a):
                return a.unsqueeze(2).to_broadcast([P, NB, NX])

            def across(a):
                return a.unsqueeze(1).to_broadcast([P, NB, NX])

            gc.then(v.tensor_reduce(MX, lg, axis=AX.X, op=ALU.max))
            v.tensor_tensor(DL, lg, wide(MX), ALU.subtract).then_inc(s_dlog, 1)
            gc.then(v.tensor_scalar(VAL, node[:, :], float(N), None, ALU.is_lt))
            gc.then(v.tensor_scalar(FARV, VAL, -FAR, FAR, ALU.mult, ALU.add))
            dve.wait_ge(s_gexp, 1)
            gc.then(v.tensor_reduce(EM, EX, axis=AX.X, op=ALU.max))
            gc.then(v.tensor_tensor(SC, EX, wide(EM), ALU.is_equal))
            gc.then(v.tensor_tensor(SC, SC, across(prefer[:, :]), ALU.mult))
            gc.then(v.tensor_reduce(SMX, SC, axis=AX.X, op=ALU.max))
            gc.then(v.tensor_tensor(SC, SC, wide(SMX), ALU.is_equal))
            v.tensor_tensor(OH, SC, wide(VAL), ALU.mult).then_inc(s_oh, 1)
            gc.then(v.tensor_reduce(SM, EX, axis=AX.X, op=ALU.add))
            gc.then(v.reciprocal(RS, SM))
            gc.then(v.tensor_tensor(GATE, EM, RS, ALU.mult))
            dve.wait_ge(s_rank, 1)
            HB = NB // 2
            for n in range(2):
                gc.then(v.tensor_copy(CNT[:, n * HB:(n + 1) * HB, :],
                                      pC[:, n * 512:n * 512 + HB * NX].rearrange("p (b e) -> p b e", e=NX)))
            for e in range(NX):
                last = v.tensor_tensor_scan(INC[:, :, e], CNT[:, :, e], CNT[:, :, e], 0.0, ALU.add, ALU.bypass)
            gc.then(last)
            gc.then(v.tensor_tensor(PL, INC, CNT, ALU.subtract))
            gc.then(v.tensor_tensor(PL, PL, across(first[:, :]), ALU.add))
            for n in range(2):
                half = PL[:, n * HB:(n + 1) * HB, :]
                gc.then(v.tensor_tensor(half, half, pB[:, n * 512:n * 512 + HB * NX]
                                        .rearrange("p (b e) -> p b e", e=NX), ALU.add))
            gc.then(v.tensor_tensor(PL, PL, OH, ALU.mult))
            gc.then(v.tensor_reduce(AT, PL, axis=AX.X, op=ALU.add))
            gc.then(v.tensor_tensor(PLACE, AT, FARV, ALU.add))

            def stage_places(b, b2):
                v.tensor_copy(pstage[:, b2:b2 + 1], PLACE[:, bass.ds(b, 1)])
                v.tensor_copy(nstage[:, b2, 0:1], node[:, bass.ds(b, 1)])
                v.tensor_copy(nstage[:, b2, 1:2].bitcast(f32), GATE[:, bass.ds(b, 1)]).then_inc(s_place, 1)

            for b2 in range(2):
                stage_places(b2, b2)

            et = Steps(dve, s_et)
            small = eneg[0:1, :]
            n_e, tiles, ends, starts = (small[:, 8 * n:8 * n + NX] for n in range(4))
            ti, tj = (small[:, 8 * n:8 * n + NX].bitcast(i32) for n in (4, 5))
            assert NX == 8
            et.then(v.tensor_scalar(n_e, INC[0:1, NB - 1, :], float(P - 1), None, ALU.add))
            et.then(v.tensor_copy(ti, n_e))
            et.then(v.tensor_scalar(tj, ti, 7, None, ALU.arith_shift_right))
            et.then(v.tensor_copy(tiles, tj))
            et.then(v.tensor_tensor_scan(ends, tiles, tiles, 0.0, ALU.add, ALU.bypass))
            et.then(v.tensor_tensor(starts, ends, tiles, ALU.subtract))
            ex, at, tmp = work[0:1, 0:NT], work[0:1, C:C + NT], work[0:1, 2 * C:2 * C + NT]
            et.then(v.memset(work[0:1, 0:2 * C], 0.0))
            for e in range(1, NX):
                et.then(v.tensor_scalar(tmp, tnum[:, :], starts[:, e:e + 1], None, ALU.is_ge))
                et.then(v.tensor_tensor(ex, ex, tmp, ALU.add))
                et.then(v.scalar_tensor_tensor(out=at, in0=tmp, scalar=starts[:, e:e + 1], in1=at,
                                               op0=ALU.mult, op1=ALU.max))
            et.then(v.tensor_tensor(tmp, tnum[:, :], at, ALU.subtract))
            et.then(v.tensor_scalar(tmp, tmp, float(P), None, ALU.mult))
            et.then(v.scalar_tensor_tensor(out=at, in0=ex, scalar=float(REG), in1=tmp, op0=ALU.mult, op1=ALU.add))
            v.tensor_scalar(etab[0:1, 0, :], ex, float(C), None, ALU.mult)
            v.tensor_copy(etab[0:1, 1, :], at).then_inc(s_etr, 1)

            with dve.Fori(0, NB // 2 - 1) as i:
                for b2 in range(2):
                    dve.wait_ge(s_list[b2], 16 * (i + 1))
                    stage_places(2 * i + 2 + b2, b2)

            dve.wait_ge(s_etr, 1)

            def copy_half(t, b2):
                dve.wait_ge(s_eT, t + 1)
                v.tensor_copy(HTx[:, b2, KH // 2:KH, :],
                              (pB, pC)[b2][:, 512:1024].rearrange("p (k n) -> p k n", k=KH // 2)).then_inc(s_eTd, 1)

            def output(t, q, need_out):
                dve.wait_ge(s_y, t + 3)
                need_out()
                v.scalar_tensor_tensor(out=obuf[:, q, :], in0=pA[:, q % 2, 0:C], scalar=ids[:, q, 1:2].bitcast(f32),
                                       in1=payx[:, q, HID:PAY], op0=ALU.mult, op1=ALU.add).then_inc(s_o, 1)

            copy_half(0, 0)
            for q in range(QB):
                copy_half(q + 1, (q + 1) % 2)
                output(q, q, lambda: None)
            with dve.Fori(1, NT // QB) as i:
                for q in range(QB):
                    t = QB * i + q
                    copy_half(t + 1, (q + 1) % 2)
                    output(t, q, lambda: dve.wait_ge(s_out[q], 16 * i))
            output(NT - 1, 0, lambda: dve.wait_ge(s_out[0], 16 * (NT // QB)))

        @block.tensor
        def _(pe):
            mm = nc.tensor.matmul
            pe.wait_ge(s_const, 2)
            pe.wait_ge(s_float, 2 + GCH)
            pe.wait_ge(s_rows, 9 * 16)
            n = 0
            for rowtable in (rrel, rsrc, rwgt):
                for c in range(GCH):
                    cnt = P if c < GCH - 1 else TAILG
                    need(pe, s_tcopied, n - 1)
                    for t in range(T):
                        at = (n % 2) * 512 + t * P
                        last = nc.tensor.transpose(pB[:, at:at + cnt], rowtable[0:cnt, c, t * P:(t + 1) * P],
                                                   ident[0:cnt, 0:cnt])
                    last.then_inc(s_tT, 1)
                    n += 1
            pe.wait_ge(s_tcopied, 3 * GCH)
            pe.wait_ge(s_regs, 1)
            pe.wait_ge(s_const, NCONST)

            for sm in (s_xT, s_hT, s_z[0], s_z[1], s_log, s_hback):
                pe.sem_inc(sm, 1)
            pe.sem_inc(s_y, 2)

            def products(slot, Sx, to, semaphore):
                for k in range(KC):
                    for t in range(T):
                        last = mm(to[:, k * W:(k + 1) * W], rows[:, slot, t, k * P:(k + 1) * P], Sx[:, t, :],
                                  start=(t == 0), stop=(t == T - 1))
                last.then_inc(semaphore, 1)

            def z_part(layer, j):
                wg, bat = ((wg1, 0), (wg2, C))[layer]
                pe.wait_ge(s_stage[layer], j + 2)
                pe.wait_ge((s_elu[0], s_zused)[layer], j + 2)
                mm(pZ[:, 0:C], ones[0:1, :], brow[0:1, bat:bat + C], start=True, stop=False)
                for k in range(KC):
                    last = mm(pZ[:, 0:C], stage[:, k, :], wg[:, k, :], start=False, stop=(k == KC - 1))
                last.then_inc(s_z[layer], 1)

            def tick1(j):
                z_part(0, j)

            def tick2(j):
                if flows(4, j - 1):
                    pe.wait_ge(s_gelu, j + 1)
                pe.wait_ge(s_payc, j + 1)
                for m in range(KH):
                    last = nc.tensor.transpose(pC[:, m * P:(m + 1) * P], HT[:, m, :], ident[:, :])
                last.then_inc(s_hback, 1)
                if flows(3, j):
                    pe.wait_ge(s_xTc, j + 2)
                pe.wait_ge(s_lg, j + 1)
                mm(pLG, ones[0:1, :], brow[0:1, 2 * C:2 * C + NX], start=True, stop=False)
                for m in range(KH):
                    last = mm(pLG, HT[:, m, :], wgate[:, m, :], start=False, stop=(m == KH - 1))
                last.then_inc(s_log, 1)
                if flows(3, j):
                    pe.wait_ge(s_hb, j + 2)
                    for m in range(KH):
                        for k in range(KC):
                            last = mm(pB[:, m * P:(m + 1) * P], w1[:, k, m * P:(m + 1) * P], xnT[:, k, :],
                                      start=(k == 0), stop=(k == KC - 1))
                    last.then_inc(s_hT, 1)
                if flows(0, j):
                    z_part(1, j)
                if flows(2, j):
                    pe.wait_ge(s_xn2, j + 2)
                    for k in range(KC):
                        last = nc.tensor.transpose(pT[:, k * P:(k + 1) * P], xn2[:, k * P:(k + 1) * P], ident[:, :])
                    last.then_inc(s_xT, 1)

            def edges_half(layer, i, h, half, with_overflow):
                for u in range(HALF):
                    s, g = half * HALF + u, HALF * h + u
                    pe.wait_ge(s_gath[layer][s], 16 * T * (i + 1))
                    if with_overflow:
                        ws, we = overflow_windows(pe, g)
                        with pe.If(ws < we):
                            with pe.Fori(ws, we) as w:
                                pe.wait_ge(s_ovS[layer], w + 1)
                                products(s, Sov, pOV, s_ovmm[layer])
                    pe.wait_ge(s_S[layer], g + 1)
                    pe.wait_ge(s_add[layer], g + 1)
                    products(s, S[:, s % 2, :, :], pA[:, s % 2, :], s_mm[layer])

            pe.wait_ge(s_w, 8 * 16)
            for layer in range(2):
                pe.sem_inc(s_mm[layer], SLOTS)
                with pe.Fori(0, ITERS) as i:
                    for half in range(2):
                        h = 2 * i + half
                        ovf, start, end = half_flags(pe, h)
                        with pe.If(ovf > 0):
                            edges_half(layer, i, h, half, True)
                        with pe.Else():
                            edges_half(layer, i, h, half, False)
                        ticks(pe, start, end, (tick1, tick2)[layer])
            for j in range(NB, NB + DEPTH):
                tick2(j)

            pe.wait_ge(s_oh, 1)
            pe.wait_ge(s_payc, NB + DEPTH + 1)
            pe.wait_ge(s_hb, NB + 5)
            HB = NB // 2
            for to, what in ((pB, before), (pC, ones)):
                for n in range(2):
                    last = mm(to[:, n * 512:n * 512 + HB * NX], what[:, :],
                              gate(3)[:, n * HB:(n + 1) * HB, :].rearrange("p b e -> p (b e)"), start=True, stop=True)
            last.then_inc(s_rank, 1)

            pe.wait_ge(s_wd, 16 * (KH + 1))
            pe.wait_ge(s_etr, 1)

            def transpose_tile(i, q):
                pe.wait_ge(s_pg[q], 16 * (i + 1))
                for m in range(KH):
                    last = nc.tensor.transpose((pB, pC)[q % 2][:, m * P:(m + 1) * P],
                                               payx[:, q, m * P:(m + 1) * P], ident[:, :])
                last.then_inc(s_eT, 1)

            def expert(t, q):
                ec = pe.value_load(etab[0:1, 0, bass.ds(t, 1)], min_val=0, max_val=(NX - 1) * C)
                pe.wait_ge(s_o, t + 1)
                mm(pA[:, q % 2, 0:C], ones[0:1, :], bd[0:1, bass.ds(ec, C)], start=True, stop=False)
                pe.wait_ge(s_eTa, t + 1)
                pe.wait_ge(s_eTd, t + 1)
                for m in range(KH):
                    last = mm(pA[:, q % 2, 0:C], HTx[:, q % 2, m, :], wdk[:, m, bass.ds(ec, C)],
                              start=False, stop=(m == KH - 1))
                last.then_inc(s_y, 1)

            transpose_tile(0, 0)
            with pe.Fori(0, NT // QB) as i:
                for q in range(QB):
                    transpose_tile(i + (q + 1) // QB, (q + 1) % QB)
                    expert(QB * i + q, q)
            expert(NT - 1, 0)


_INS = ['x', 'src', 'dst', 'edge_weight', 'L0_gnn_W1', 'L0_gnn_b1', 'L0_gnn_W2', 'L0_gnn_b2',
        'L0_ffn_W1', 'L0_ffn_b1', 'L0_ffn_Wg', 'L0_ffn_bg', 'L0_ffn_Wd', 'L0_ffn_bd']


def kernel(**inputs):
    import numpy as _np
    import concourse.bacc as _bacc
    from concourse import mybir as _mybir
    from concourse.bass_utils import run_bass_kernel_spmd as _run

    nc = _bacc.Bacc("TRN2", target_bir_lowering=False, num_devices=1)
    arrays, args = {}, []
    for name in _INS:
        a = _np.ascontiguousarray(inputs[name])
        arrays[f"in_{name}_dram"] = a
        args.append(nc.dram_tensor(f"in_{name}_dram", a.shape, _mybir.dt.from_np(a.dtype), kind="ExternalInput").ap())
    args.append(nc.dram_tensor("out_0_dram", inputs['x'].shape, _mybir.dt.float32, kind="ExternalOutput").ap())
    bass_gnn_then_routed_ffn(nc, *args)
    nc.compile()
    r = _run(nc, [arrays], core_ids=[0])
    return r.results[0]["out_0_dram"]
```

```python
import concourse.bass as bass
from concourse import mybir
from contextlib import ExitStack

P = 128


def bass_gnn_then_routed_ffn(
    nc: bass.Bass,
    x: bass.AP,
    src: bass.AP,
    dst: bass.AP,
    edge_weight: bass.AP,
    gnn_W1: bass.AP,
    gnn_b1: bass.AP,
    gnn_W2: bass.AP,
    gnn_b2: bass.AP,
    ffn_W1: bass.AP,
    ffn_b1: bass.AP,
    ffn_Wg: bass.AP,
    ffn_bg: bass.AP,
    ffn_Wd: bass.AP,
    ffn_bd: bass.AP,
    out: bass.AP,
):
    f32, i32 = mybir.dt.float32, mybir.dt.int32
    ALU, ACT, AX = mybir.AluOpType, mybir.ActivationFunctionType, mybir.AxisListType

    N, C = x.shape
    E = dst.shape[0]
    HID = ffn_W1.shape[1]
    NX = ffn_Wg.shape[1]
    KC = C // P
    KH = HID // P
    T = 4
    GE = T * P
    W = 96
    SLOTS = 8
    HALF = SLOTS // 2
    ITERS = -(-E // (GE * SLOTS))
    NG = ITERS * SLOTS
    NH = NG // HALF
    NB = -(-N // P)
    LAST = N - (NB - 1) * P
    NPAD = NB * P
    LEAD = 2
    DEPTH = 5
    AGG = NPAD + W
    GCH = -(-NG // P)
    TBL = NG + 8
    FULL_ROWS = E // GE
    LAST_EDGES = E - FULL_ROWS * GE
    BODY = (GCH - 1) * P
    TAILG = NG - BODY
    NT = NB + NX - 1
    QB = 4
    RING = 2 * QB
    LB = 7
    PAY = HID + C
    FAR = float(NT * P)
    PG = P + NX
    PERB = 512 // PG
    FUSED = 2 * PERB
    EPS = 1e-5
    PACK = 14
    KWIN = (N - 1) // W
    LNC = NB // T
    LNI = LNC // SLOTS
    LNB = 4
    LTAIL = NB - LNC * T
    assert NH - 1 + LEAD >= NB
    assert SLOTS == 2 * HALF and HALF == 4 and NB < 256 and NPAD < (1 << PACK)
    assert NB % (2 * LB) == 0 and C + (KH - FUSED) * P <= 512 and 0 < TAILG <= 32 and FULL_ROWS > BODY
    assert LNC == LNI * SLOTS and SLOTS % LNB == 0 and 3 * GCH <= LNC and LTAIL == 2 and NT % RING == 1 and NH < P

    xn_d = nc.dram_tensor("xn_scratch", [N, C], f32, kind="Internal").ap()
    h1_d = nc.dram_tensor("h1_scratch", [NPAD, C], f32, kind="Internal").ap()
    pay_d = nc.dram_tensor("pay_scratch", [NPAD, PAY], f32, kind="Internal").ap()

    ctx = ExitStack()
    with ctx:
        def sb(name, shape, dt=f32):
            return ctx.enter_context(nc.sbuf_tensor(name, shape, dt))

        def ps(name, shape):
            return ctx.enter_context(nc.psum_tensor(name, shape, f32))

        def sem(name):
            return ctx.enter_context(nc.semaphore(name))

        aggT = sb("aggT", [P, KC, AGG])
        rows = sb("rows", [P, SLOTS, T, C])
        tdst = sb("tdst", [P, T, TBL])
        twgt = sb("twgt", [P, T, TBL])
        tsrc = sb("tsrc", [P, T, TBL])
        idx = sb("idx", [P, 2, HALF, T], i32)
        S = sb("S", [P, 2, T, W])
        Sov = sb("Sov", [P, T, W])
        cur = sb("cur", [P, T])
        woff = sb("woff", [P, KWIN + 1])
        regs = sb("regs", [1, NH, 4], i32)
        wins = sb("wins", [1, NG, 2], i32)
        wg1 = sb("wg1", [P, KC, C])
        wg2 = sb("wg2", [P, KC, C])
        w1 = sb("w1", [P, KC, HID])
        identg = sb("identg", [P, KH, PG])
        b1col = sb("b1col", [P, KH])
        brow = sb("brow", [P, 2 * C + NX])
        zb = sb("zb", [P, C])
        ident = sb("ident", [P, P])
        flip = sb("flip", [P, P])
        ones = sb("ones", [P, P])
        before = sb("before", [P, P])
        iota_w = sb("iota_w", [P, W])
        stats = sb("stats", [P, LNB, T, 6])
        mv = sb("mv", [P, LNB, T, 2])
        std = sb("std", [P, LNB, T])
        rstd = sb("rstd", [P, LNB, T])
        nmr = sb("nmr", [P, LNB, T])
        zeros = sb("zeros", [P, KC, P])
        stage = sb("stage", [P, KC, P])
        zneg = sb("zneg", [P, C])
        zexp = sb("zexp", [P, C])
        work = sb("work", [P, 16 * C])
        HT = work[:, 0:HID].rearrange("p (k n) -> p k n", k=KH)
        hid = work[:, HID:2 * HID].rearrange("p (k n) -> p k n", k=KH)
        payh = work[:, 2 * HID:3 * HID]
        w0 = 3 * HID
        xnT = work[:, w0:w0 + C].rearrange("p (k n) -> p k n", k=KC)
        xn2, x1, xb = (work[:, w0 + C * n:w0 + C * (n + 1)] for n in (1, 2, 3))
        hout = payh[:, 0:C]
        bstat = sb("bstat", [P, 6])
        bmv = sb("bmv", [P, 2])
        bstd = sb("bstd", [P, 2])
        lgpart = sb("lgpart", [P, 2, NX])
        LG = sb("LG", [P, NB + DEPTH, NX])
        epsc = sb("epsc", [P, 1])
        prefer = sb("prefer", [P, NX])
        tnum = sb("tnum", [P, NT])
        iota_p = sb("iota_p", [P, P])
        node = sb("node", [P, NB])
        lists = sb("lists", [P, 2, NT])
        ids = sb("ids", [P, RING], i32)
        etab = sb("etab", [1, NT], i32)
        flat = aggT[:, :, :].rearrange("p k n -> p (k n)")
        RW = GCH * GE

        def table(n, dt=f32):
            v = flat[:, n * RW:(n + 1) * RW]
            return (v if dt is f32 else v.bitcast(dt)).rearrange("p (c e) -> p c e", c=GCH)

        rdst_i, rsrc_i, rwgt, rdst, rsrc, rrel = table(0, i32), table(1, i32), table(2), table(3), table(4), table(5)

        def gvec(n, dt=f32):
            v = flat[:, 6 * RW + n * GCH:6 * RW + (n + 1) * GCH]
            return v if dt is f32 else v.bitcast(dt)

        def grow(n, dt=f32):
            v = work[0:1, n * GCH * P:(n + 1) * GCH * P]
            return v if dt is f32 else v.bitcast(dt)

        rflat = rows[:, :, :, :].rearrange("p s t c -> p (s t c)")

        def gate(n):
            return rflat[:, n * NB * NX:(n + 1) * NB * NX].rearrange("p (b e) -> p b e", e=NX)

        def per_node(n):
            return rflat[:, 7 * NB * NX + n * NB:7 * NB * NX + (n + 1) * NB]

        wdk = flat[:, 0:NX * KH * C].rearrange("p (k xc) -> p k xc", k=KH)
        o1 = NX * KH * C
        bd = flat[:, o1:o1 + NX * C]
        o2 = o1 + NX * C
        obuf = flat[:, o2:o2 + QB * C].rearrange("p (b c) -> p b c", b=QB)
        payx = flat[:, o2 + QB * C:o2 + QB * C + QB * PAY].rearrange("p (b f) -> p b f", b=QB)
        o3 = o2 + QB * C
        lane_is = flat[:, o3:o3 + 2 * LB * P].rearrange("p (s b n) -> p s b n", s=2, b=LB)
        o4 = o3 + 2 * LB * P
        in_tile = work[:, 0:2 * LB * NT].rearrange("p (s b n) -> p s b n", s=2, b=LB)
        tile_is = flat[:, o4:o4 + 4 * LB * NT].rearrange("p (s b v n) -> p s b v n", s=2, b=LB, v=2)
        HTx = work[:, 0:2 * HID].rearrange("p (b k n) -> p b k n", b=2, k=KH)
        assert max(o3 + QB * PAY, o4 + 4 * LB * NT) <= KC * AGG and 6 * RW + 8 * GCH <= KC * AGG
        assert 8 * GCH * P <= 16 * C and 7 * NB * NX + 16 * NB <= SLOTS * T * C

        pA = ps("pA", [P, 2, 512])
        pZ = ps("pZ", [P, 512])
        pT = ps("pT", [P, 512])
        pB = ps("pB", [P, 1024])
        pC = ps("pC", [P, 1024])
        pOV = pZ[:, C:C + KC * W]
        pROW = (pC[0:1, 0:NG], pC[0:1, 512:512 + NG], pT[0:1, 0:NG])
        pL = pT[:, 0:2 * NT]
        pF = pC[:, :].rearrange("p (b n) -> p b n", b=2)[:, :, 0:PERB * PG].rearrange("p b (c g) -> p b c g", g=PG)
        pLG = pA[:, 1, KC * W:KC * W + NX]

        block = ctx.enter_context(nc.Block())

        s_held = {e.engine: sem(f"held_{n}") for n, e in
                  (("sync", nc.sync), ("pool", nc.gpsimd), ("dve", nc.vector), ("act", nc.scalar))}
        s_const = sem("constants_ready")
        NCONST = 12
        s_rows_clear = sem("edge_rows_padded")
        s_rows = sem("edge_rows_loaded")
        s_w = sem("weights_loaded")
        s_tchain = sem("dve_table_step")
        s_float = sem("edge_rows_float")
        s_tT = sem("table_transposed")
        s_tcopied = sem("table_copied")
        s_gvec = sem("group_vectors_ready")
        s_grow = sem("group_rows_ready")
        s_regs = sem("register_table_ready")
        s_tbl_clear = sem("tables_cleared")
        s_xin = [sem(f"x_loaded_{i}") for i in range(SLOTS)]
        s_xst = [sem(f"xn_stored_{i}") for i in range(SLOTS)]
        s_ln = sem("dve_layernorm_step")
        s_var = sem("variance_ready")
        s_std = sem("std_ready")
        s_nmr = sem("layernorm_scales_ready")
        s_nd = sem("normalised_by_dve")
        s_na = sem("normalised_by_act")
        s_np = sem("normalised_by_pool")
        s_aggclear = sem("aggT_cleared")
        s_blkclear = sem("aggT_block_cleared")
        s_idx = [sem(f"indices_staged_{l}") for l in range(2)]
        s_gath = [[sem(f"rows_gathered_{l}_{i}") for i in range(SLOTS)] for l in range(2)]
        s_S = [sem(f"S_ready_{l}") for l in range(2)]
        s_mm = [sem(f"group_multiplied_{l}") for l in range(2)]
        s_add = [sem(f"group_added_{l}") for l in range(2)]
        s_ovS = [sem(f"overflow_S_ready_{l}") for l in range(2)]
        s_ovmm = [sem(f"overflow_multiplied_{l}") for l in range(2)]
        s_ovadd = [sem(f"overflow_added_{l}") for l in range(2)]
        s_ovc = [sem(f"overflow_window_moved_{l}") for l in range(2)]
        s_stage = [sem(f"block_staged_{l}") for l in range(2)]
        s_z = [sem(f"Z_ready_{l}") for l in range(2)]
        s_zexp = [sem(f"Z_exp_ready_{l}") for l in range(2)]
        s_zb = [sem(f"Z_biased_{l}") for l in range(2)]
        s_zneg = [sem(f"Z_negative_part_{l}") for l in range(2)]
        s_elu = [sem(f"elu_ready_{l}") for l in range(2)]
        s_free = [sem(f"elu_store_done_{l}") for l in range(2)]
        s_eln = [sem(f"elu_step_{l}") for l in range(2)]
        s_h1st = sem("h1_stored")
        s_x1st = sem("x1_stored")
        s_xb = sem("x_block_loaded")
        s_tick = sem("dve_tick_step")
        s_var2 = sem("block_variance_ready")
        s_std2 = sem("block_std_ready")
        s_xn2 = sem("block_normalised")
        s_xT = sem("block_transposed")
        s_xTc = sem("block_transpose_copied")
        s_hT = sem("hidden_ready")
        s_hb = sem("hidden_biased")
        s_gelu = sem("hidden_activated")
        s_log = sem("logits_ready")
        s_lgp = sem("logits_parts_ready")
        s_lg = sem("logits_copied")
        s_hback = sem("hidden_transposed_back")
        s_payc = sem("hidden_rows_copied")
        s_payst = sem("hidden_rows_stored")
        s_payfree = sem("hidden_rows_store_done")
        s_gate = sem("dve_gate_step")
        s_dlog = sem("logits_less_max_ready")
        s_gexp = sem("gate_exp_ready")
        s_oh = sem("choice_ready")
        s_rank = sem("ranks_ready")
        s_in = sem("in_tile_ready")
        s_tile = sem("place_matrices_ready")
        s_tgate = sem("gate_matrices_ready")
        s_lmm = sem("list_products_done")
        s_wd = sem("expert_weights_loaded")
        s_et = sem("dve_expert_table_step")
        s_etr = sem("expert_table_ready")
        s_ids = sem("ids_staged")
        s_pg = [sem(f"payload_gathered_{i}") for i in range(QB)]
        s_eT = sem("expert_tile_transposed")
        s_eTa = sem("expert_tile_copied_by_act")
        s_eTd = sem("expert_tile_copied_by_dve")
        s_y = sem("expert_output_ready")
        s_yb = sem("expert_output_biased")
        s_o = sem("output_tile_ready")
        s_out = [sem(f"output_scattered_{i}") for i in range(QB)]

        def need(eng, semaphore, value):
            if isinstance(value, int) and value < 1:
                return
            eng.wait_ge(semaphore, value)

        def hold(eng, semaphore, value):
            if isinstance(value, int) and value < 1:
                return
            eng.wait_ge(semaphore, value)
            if not isinstance(value, int):
                eng.sem_inc(s_held[eng.engine], 1)

        class Steps:

            def __init__(self, eng, semaphore):
                self.eng, self.sem, self.base, self.n = eng, semaphore, 0, 0

            def then(self, ins, own=False):
                self.n += 1
                ins.then_inc(self.sem, 1)
                (hold if own else need)(self.eng, self.sem, self.base + self.n)

        def within(value, low, high):
            return nc.s_assert_within(value, low, high, skip_runtime_bounds_check_because=
                                      "windows end at the group's largest dst, which is below the number of nodes")

        def runs(eng, count):
            yield 0
            with eng.Fori(1, count - 1) as i:
                yield i
            yield count - 1

        def block_of(j):
            return bass.ds(j * -P + (NB - 1) * P, P)

        def flows(k, j):
            return not isinstance(j, int) or j - k < NB

        def half_flags(eng, h):
            v = eng.value_load(regs[0:1, bass.ds(h, 1), 0], min_val=0, max_val=(1 << 17) - 1)
            return v >> 16, (v >> 8) & 255, v & 255

        def overflow_windows(eng, g):
            ws = eng.value_load(wins[0:1, bass.ds(g, 1), 0], min_val=0, max_val=NG * P)
            we = eng.value_load(wins[0:1, bass.ds(g, 1), 1], min_val=0, max_val=NG * P)
            return ws, we

        def ticks(eng, start, end, tick):
            with eng.If(start < end):
                with eng.Fori(start, end) as j:
                    tick(nc.s_assert_within(j, 0, NB - 1, skip_runtime_bounds_check_because=
                                            "the table's last end is the number of blocks"))

        @block.sync
        def _(sp):
            def x_chunk(c):
                return x[bass.ds(c * (T * P), T * P), :].rearrange("(t p) f -> p t f", p=P)

            def xn_chunk(c):
                return xn_d[bass.ds(c * (T * P), T * P), :].rearrange("(t p) f -> p t f", p=P)

            AHEAD = SLOTS - 2
            for c in range(2):
                sp.dma_start(rows[:, c, :, :], x_chunk(c)).then_inc(s_xin[c], 16)
            sp.wait_ge(s_rows_clear, 3)
            for to, frm in ((rdst_i, dst), (rsrc_i, src), (rwgt, edge_weight)):
                sp.dma_start(to[:, 0:GCH - 1, :],
                             frm[0:BODY * GE].rearrange("(c p e) -> p c e", p=P, e=GE)).then_inc(s_rows, 16)
                sp.dma_start(to[0:FULL_ROWS - BODY, GCH - 1, :],
                             frm[BODY * GE:FULL_ROWS * GE].rearrange("(p e) -> p e", e=GE)).then_inc(s_rows, 16)
                sp.dma_start(to[FULL_ROWS - BODY:FULL_ROWS - BODY + 1, GCH - 1, 0:LAST_EDGES],
                             frm[FULL_ROWS * GE:E].rearrange("(a e) -> a e", a=1)).then_inc(s_rows, 16)
            for c in range(2, AHEAD):
                sp.dma_start(rows[:, c, :, :], x_chunk(c)).then_inc(s_xin[c], 16)
            for i in runs(sp, LNI):
                for s in range(SLOTS):
                    c = SLOTS * i + s
                    to = (s + AHEAD) % SLOTS
                    if not isinstance(i, int) or c + AHEAD <= LNC:
                        need(sp, s_xst[to], 16 * (i + 1 if s >= 2 else i))
                        if isinstance(i, int) and c + AHEAD == LNC:
                            sp.dma_start(rows[:, to, 0, :], x[LNC * T * P:(NB - 1) * P, :]).then_inc(s_xin[to], 16)
                            sp.dma_start(rows[0:LAST, to, 1, :], x[(NB - 1) * P:N, :]).then_inc(s_xin[to], 16)
                        else:
                            sp.dma_start(rows[:, to, :, :], x_chunk(c + AHEAD)).then_inc(s_xin[to], 16)
                    sp.wait_ge(s_nd, c + 1)
                    sp.wait_ge(s_na, c + 1)
                    sp.wait_ge(s_np, c + 1)
                    sp.dma_start(xn_chunk(c), rows[:, s, :, :]).then_inc(s_xst[s], 16)
            sp.wait_ge(s_nd, LNC + 1)
            sp.wait_ge(s_na, LNC + 1)
            sp.dma_start(xn_d[LNC * T * P:(NB - 1) * P, :], rows[:, 0, 0, :]).then_inc(s_xst[0], 16)
            sp.dma_start(xn_d[(NB - 1) * P:N, :], rows[0:LAST, 0, 1, :]).then_inc(s_xst[0], 16)

            for to, frm in ((wg1, gnn_W1), (wg2, gnn_W2), (w1, ffn_W1),
                            (identg[:, :, P:PG], ffn_Wg)):
                sp.dma_start(to[:, :, :], frm.rearrange("(k p) n -> p k n", p=P)).then_inc(s_w, 16)
            for at, frm in ((0, gnn_b1), (C, gnn_b2), (2 * C, ffn_bg)):
                n = frm.shape[0]
                sp.dma_start(brow[:, at:at + n], frm.rearrange("(a n) -> a n", a=1).to_broadcast([P, n]))\
                  .then_inc(s_w, 16)
            with nc.allow_non_contiguous_dma(reason="1024 bias values, once"):
                sp.dma_start(b1col[:, :], ffn_b1.rearrange("(k p) -> p k", p=P)).then_inc(s_w, 16)

            sp.sem_inc(s_free[0], 1)
            sp.wait_ge(s_elu[0], 2)
            sp.sem_inc(s_free[0], 1)
            with sp.Fori(0, NB) as b:
                sp.wait_ge(s_elu[0], b + 3)
                sp.dma_start(h1_d[block_of(b), :], hout).then_inc(s_h1st, 16)
                sp.wait_ge(s_h1st, 16 * (b + 1))
                sp.sem_inc(s_free[0], 1)

            sp.sem_inc(s_free[1], 1)
            sp.sem_inc(s_payfree, 1)
            sp.wait_ge(s_elu[1], 1)

            def load_x(j):
                if isinstance(j, int) and j == 0:
                    sp.dma_start(xb[0:LAST, :], x[(NB - 1) * P:N, :]).then_inc(s_xb, 16)
                else:
                    sp.dma_start(xb, x[block_of(j), :]).then_inc(s_xb, 16)

            load_x(0)

            def blocks_io(j, load=None, x1_rows=True, hidden_rows=True):
                if x1_rows or load is not None:
                    sp.wait_ge(s_elu[1], j + 2)
                if load is not None:
                    load()
                if x1_rows:
                    sp.dma_start(pay_d[block_of(j - 1), HID:PAY], x1).then_inc(s_x1st, 16)
                    sp.wait_ge(s_x1st, 16 * j)
                sp.sem_inc(s_free[1], 1)
                sp.wait_ge(s_payc, j + 2)
                if hidden_rows:
                    sp.dma_start(pay_d[block_of(j - DEPTH), 0:HID], payh).then_inc(s_payst, 16)
                    sp.wait_ge(s_payst, 16 * (j - DEPTH + 1))
                sp.sem_inc(s_payfree, 1)

            for j in range(DEPTH):
                blocks_io(j, lambda: load_x(j), x1_rows=j > 0, hidden_rows=False)
            with sp.Fori(DEPTH, NB) as j:
                blocks_io(j, lambda: load_x(j))
            for j in range(NB, NB + DEPTH):
                blocks_io(j, x1_rows=j == NB)

            sp.wait_ge(s_stage[1], NB + 1)
            for k in range(KH):
                sp.dma_start(wdk[:, k, :].rearrange("p (x c) -> p x c", x=NX),
                             ffn_Wd[:, k * P:(k + 1) * P, :].rearrange("x p c -> p x c")).then_inc(s_wd, 16)
            sp.dma_start(bd, ffn_bd.rearrange("x (a c) -> a (x c)", a=1).to_broadcast([P, NX * C])).then_inc(s_wd, 16)

            sp.wait_ge(s_out[0], 16 * (NT // QB + 1))
            for q in range(1, QB):
                sp.wait_ge(s_out[q], 16 * (NT // QB))

        @block.gpsimd
        def _(pool):
            pool.memset(rdst_i[0:TAILG, GCH - 1, :], N - 1).then_inc(s_rows_clear, 1)
            pool.memset(rsrc_i[0:TAILG, GCH - 1, :], 0).then_inc(s_rows_clear, 1)
            pool.memset(rwgt[0:TAILG, GCH - 1, :], 0.0).then_inc(s_rows_clear, 1)
            pool.memset(ones[:, :], 1.0).then_inc(s_const, 1)
            pool.wait_ge(s_const, 1)
            pool.affine_select(out=ident[:, :], in_=ones[:, :], compare_op=ALU.is_equal, fill=0.0, base=0,
                               pattern=[[-1, P]], channel_multiplier=1).then_inc(s_const, 1)
            pool.affine_select(out=flip[:, :], in_=ones[:, :], compare_op=ALU.is_equal, fill=0.0, base=-(P - 1),
                               pattern=[[1, P]], channel_multiplier=1).then_inc(s_const, 1)
            pool.affine_select(out=before[:, :], in_=ones[:, :], compare_op=ALU.is_gt, fill=0.0, base=0,
                               pattern=[[1, P]], channel_multiplier=-1).then_inc(s_const, 1)
            for t in (tdst, twgt, tsrc):
                pool.memset(t[:, :, NG:TBL], 0.0).then_inc(s_tbl_clear, 1)
            for to, pattern, base, per_lane in ((iota_w, [[1, W]], 0, 0), (woff, [[W, KWIN + 1]], 0, 0),
                                                (prefer, [[-1, NX]], NX, 0), (iota_p, [[1, P]], 0, 0),
                                                (tnum, [[1, NT]], 0, 0), (node, [[P, NB]], 0, 1)):
                pool.iota(to[:, :], pattern, base=base, channel_multiplier=per_lane,
                          allow_small_or_imprecise_dtypes=True).then_inc(s_const, 1)
            pool.memset(zeros[:, :, :], 0.0).then_inc(s_const, 1)

            for i in runs(pool, LNI):
                for s in range(SLOTS):
                    c = SLOTS * i + s
                    hold(pool, s_nmr, c + 1)
                    pool.tensor_scalar(rows[:, s, T - 1, :], rows[:, s, T - 1, :], mv[:, s % LNB, T - 1, 0:1],
                                       rstd[:, s % LNB, T - 1:T], ALU.subtract, ALU.mult).then_inc(s_np, 1)

            for layer, source in ((0, xn_d), (1, h1_d)):
                if layer == 0:
                    pool.wait_ge(s_xst[0], 16 * (LNI + 2))
                    for s in range(1, SLOTS):
                        pool.wait_ge(s_xst[s], 16 * LNI)
                else:
                    pool.wait_ge(s_h1st, 16 * NB)
                with pool.Fori(0, ITERS) as i:
                    for s in range(SLOTS):
                        g = SLOTS * i + s
                        if s % HALF == 0:
                            hold(pool, s_idx[layer], 2 * i + s // HALF + 1)
                        hold(pool, s_mm[layer], g + 1)
                        for t in range(T):
                            at = idx[:, s // HALF, s % HALF, t:t + 1]
                            pool.indirect_dma_start(rows[:, s, t, :], None, source,
                                                    bass.IndirectOffsetOnAxis(at, 0))\
                                .then_inc(s_gath[layer][s], 16)

            for i in runs(pool, NB // (2 * LB)):
                for n in range(2):
                    c = 2 * i + n
                    hold(pool, s_lmm, c - 1)
                    hold(pool, s_in, c + 1)
                    pool.tensor_tensor(tile_is[:, n, :, 1, :], in_tile[:, n, :, :],
                                       per_node(4)[:, bass.ds(c * LB, LB)].unsqueeze(2).to_broadcast([P, LB, NT]),
                                       ALU.mult).then_inc(s_tgate, 1)

            pool.wait_ge(s_payst, 16 * NB)
            pool.wait_ge(s_x1st, 16 * NB)

            def gather(t, q, r):
                hold(pool, s_ids, t + 1)
                pool.indirect_dma_start(payx[:, q, :], None, pay_d,
                                        bass.IndirectOffsetOnAxis(ids[:, r:r + 1], 0)).then_inc(s_pg[q], 16)

            def scatter(t, q, r):
                hold(pool, s_o, t + 3)
                pool.indirect_dma_start(out, bass.IndirectOffsetOnAxis(ids[:, r:r + 1], 0), obuf[:, q, :],
                                        None, bounds_check=N - 1, oob_is_err=False).then_inc(s_out[q], 16)

            for q in range(QB):
                gather(q, q, q)
            for i in runs(pool, NT // RING):
                for r in range(RING):
                    t = RING * i + r
                    scatter(t, r % QB, r)
                    if not isinstance(t, int) or t + QB < NT:
                        gather(t + QB, r % QB, (r + QB) % RING)
            scatter(NT - 1, 0, 0)

        @block.scalar
        def _(act):
            def copy_table(n):
                c = n % GCH
                cnt = P if c < GCH - 1 else TAILG
                act.wait_ge(s_tT, n + 1)
                at = NG - c * P - cnt
                act.activation((tdst, tsrc, twgt)[n // GCH][:, :, at:at + cnt],
                               pB[:, (n % 2) * 512:(n % 2 + 1) * 512].rearrange("p (t g) -> p t g", t=T)[:, :, 0:cnt],
                               ACT.Copy).then_inc(s_tcopied, 1)

            def root(c, par, n):
                act.wait_ge(s_var, c + 1)
                act.activation(std[:, par, 0:n], mv[:, par, 0:n, 1], ACT.Sqrt, bias=epsc[:, :]).then_inc(s_std, 1)

            def normalise(c, slot, par, n):
                act.wait_ge(s_nmr, c + 1)
                for t in range(1, max(n - 1, 2)):
                    last = act.activation(rows[:, slot, t, :], rows[:, slot, t, :], ACT.Identity,
                                          bias=nmr[:, par, t:t + 1], scale=rstd[:, par, t:t + 1])
                last.then_inc(s_na, 1)

            for i in runs(act, LNI):
                for s in range(SLOTS):
                    c = SLOTS * i + s
                    root(c, s % LNB, T)
                    if isinstance(c, int) and c >= LNC - 3 * GCH:
                        copy_table(c - (LNC - 3 * GCH))
                    if not (isinstance(c, int) and c == 0):
                        normalise(c - 1, (s - 1) % SLOTS, (s - 1) % LNB, T)
            root(LNC, 0, LTAIL)
            normalise(LNC - 1, SLOTS - 1, LNB - 1, T)
            normalise(LNC, 0, 0, LTAIL)

            act.wait_ge(s_tcopied, 3 * GCH)
            act.wait_ge(s_const, NCONST)
            act.wait_ge(s_grow, 1)
            act.activation(aggT[:, 1, :], zeros[:, 0, 0:1].to_broadcast([P, AGG]), ACT.Copy).then_inc(s_aggclear, 1)
            act.wait_ge(s_regs, 1)

            def stage_block(layer, j, h):
                act.wait_ge(s_add[layer], HALF * (h + 1) + 2)
                hold(act, s_z[layer], j + 1)
                act.activation(stage[:, :, :], aggT[:, :, block_of(j)],
                               ACT.Copy).then_inc(s_stage[layer], 1)

            def exponent(layer, j):
                act.wait_ge(s_zb[layer], j + 2)
                act.wait_ge(s_elu[layer], j + 1)
                act.activation(zneg[:, :], zb[:, :], ACT.Relu, scale=-1.0).then_inc(s_zneg[layer], 1)
                act.wait_ge(s_zneg[layer], j + 1)
                act.activation(zexp[:, :], zneg[:, :], ACT.Exp, scale=-1.0).then_inc(s_zexp[layer], 1)

            def tick1(j, h):
                if flows(0, j):
                    stage_block(0, j, h)
                exponent(0, j)
                if flows(0, j):
                    hold(act, s_stage[0], j + 2)
                    act.activation(aggT[:, :, block_of(j)], zeros[:, :, :], ACT.Copy).then_inc(s_blkclear, 1)

            def tick2(j, h):
                if flows(0, j):
                    stage_block(1, j, h)
                if flows(1, j):
                    exponent(1, j)
                if flows(2, j):
                    act.wait_ge(s_var2, j + 1)
                    act.wait_ge(s_xn2, j + 1)
                    act.activation(bstd[:, 0:1], bmv[:, 1:2], ACT.Sqrt, bias=epsc[:, :]).then_inc(s_std2, 1)
                act.wait_ge(s_hback, j + 2)
                act.wait_ge(s_payfree, j + 1)
                act.activation(payh[:, 0:FUSED * P].rearrange("p (b c n) -> p b c n", b=2, n=P), pF[:, :, :, 0:P],
                               ACT.Copy)
                act.activation(payh[:, FUSED * P:], pT[:, C:C + (KH - FUSED) * P], ACT.Copy).then_inc(s_payc, 1)
                if flows(4, j):
                    act.wait_ge(s_hb, j + 2)
                    act.wait_ge(s_log, j + 2)
                    act.activation(HT, hid, ACT.Gelu).then_inc(s_gelu, 1)

            for sm in (s_stage[0], s_zexp[0], s_stage[1], s_zexp[1], s_std2, s_gelu, s_payc):
                act.sem_inc(sm, 1)
            for layer in range(2):
                with act.Fori(0, ITERS) as i:
                    for half in range(2):
                        h = 2 * i + half
                        _, start, end = half_flags(act, h)
                        ticks(act, start, end, lambda j: (tick1, tick2)[layer](j, h))
                if layer == 0:
                    tick1(NB, None)
            for j in range(NB, NB + DEPTH):
                tick2(j, None)

            act.wait_ge(s_dlog, 1)
            act.activation(gate(1), gate(0), ACT.Exp).then_inc(s_gexp, 1)

            def copy_half(t, b2):
                act.wait_ge(s_eT, t + 1)
                act.wait_ge(s_y, t + 1)
                act.activation(HTx[:, b2, 0:KH // 2, :],
                               (pB, pC)[b2][:, 0:512].rearrange("p (k n) -> p k n", k=KH // 2),
                               ACT.Copy).then_inc(s_eTa, 1)

            with act.Fori(0, NT // 2) as i:
                for b2 in range(2):
                    copy_half(2 * i + b2, b2)
            copy_half(NT - 1, 0)

        @block.vector
        def _(dve):
            v = nc.vector
            tc = Steps(dve, s_tchain)
            tc.then(v.memset(epsc[:, :], EPS))

            dve.wait_ge(s_const, 3)
            v.tensor_copy(identg[:, :, 0:P], ident[:, :].unsqueeze(1).to_broadcast([P, KH, P])).then_inc(s_const, 1)

            def tables():
                dve.wait_ge(s_rows, 9 * 16)
                parts = ((P, slice(0, GCH - 1)), (TAILG, slice(GCH - 1, GCH)))
                for n, c in parts:
                    v.tensor_copy(rsrc[0:n, c, :], rsrc_i[0:n, c, :]).then_inc(s_float, 1)
                    tc.then(v.tensor_copy(rdst[0:n, c, :], rdst_i[0:n, c, :]))
                LO, HI, D, Q = gvec(0), gvec(1), gvec(2), gvec(3)
                Di, Qi, NVi = gvec(5, i32), gvec(6, i32), gvec(7, i32)
                tc.then(v.memset(flat[:, 6 * RW:6 * RW + 2 * GCH], 0.0))
                for n, c in parts:
                    v.tensor_reduce(LO[0:n, c], rdst[0:n, c, :], axis=AX.X, op=ALU.min)
                    tc.then(v.tensor_reduce(HI[0:n, c], rdst[0:n, c, :], axis=AX.X, op=ALU.max))
                for c in range(GCH):
                    n = P if c < GCH - 1 else TAILG
                    v.tensor_scalar(rrel[0:n, c, :], rdst[0:n, c, :], LO[0:n, c:c + 1], None, ALU.subtract)\
                     .then_inc(s_float, 1)
                assert W == 96
                tc.then(v.tensor_tensor(D, HI, LO, ALU.subtract))
                tc.then(v.tensor_copy(Di, D))
                tc.then(v.tensor_scalar(Qi, Di, 5, None, ALU.arith_shift_right))
                tc.then(v.tensor_copy(Q, Qi))
                tc.then(v.tensor_scalar(D, Q, 21846.0, None, ALU.mult))
                tc.then(v.tensor_copy(Di, D))
                tc.then(v.tensor_scalar(NVi, Di, 16, None, ALU.arith_shift_right))
                v.tensor_copy(Q, NVi).then_inc(s_gvec, 1)

            lnc = Steps(dve, s_ln)

            def statistics(c, slot, par, n):
                for t in range(n):
                    last = v.bn_stats(stats[:, par, t, :], rows[:, slot, t, :])
                lnc.then(last, own=True)
                for t in range(n):
                    last = v.bn_aggr(mv[:, par, t, :], stats[:, par, t, :])
                last.then_inc(s_var, 1)

            def scales(c, slot, par, n):
                dve.wait_ge(s_std, c + 1)
                lnc.then(v.reciprocal(rstd[:, par, 0:n], std[:, par, 0:n]))
                v.scalar_tensor_tensor(out=nmr[:, par, 0:n], in0=mv[:, par, 0:n, 0], scalar=-1.0,
                                       in1=rstd[:, par, 0:n], op0=ALU.mult, op1=ALU.mult).then_inc(s_nmr, 1)
                v.tensor_scalar(rows[:, slot, 0, :], rows[:, slot, 0, :], mv[:, par, 0, 0:1], rstd[:, par, 0:1],
                                ALU.subtract, ALU.mult).then_inc(s_nd, 1)

            for i in runs(dve, LNI):
                if isinstance(i, int) and i == 1:
                    tables()
                first_chunk = isinstance(i, int) and i == 0
                lnc.base, lnc.n = 0 if first_chunk else 2 * SLOTS * i - 1, 0
                for s in range(SLOTS):
                    c = SLOTS * i + s
                    dve.wait_ge(s_xin[s], 16 * (i + 1))
                    need(dve, s_na, c - (LNB - 1))
                    need(dve, s_np, c - (LNB - 1))
                    statistics(c, s, s % LNB, T)
                    if s or not first_chunk:
                        scales(c - 1, (s - 1) % SLOTS, (s - 1) % LNB, T)
            lnc.base, lnc.n = 2 * LNC - 1, 0
            dve.wait_ge(s_xin[0], 16 * (LNI + 2))
            dve.wait_ge(s_na, LNC - (LNB - 1))
            dve.wait_ge(s_np, LNC - (LNB - 1))
            statistics(LNC, 0, 0, LTAIL)
            scales(LNC - 1, SLOTS - 1, LNB - 1, T)
            scales(LNC, 0, 0, LTAIL)

            def stage_idx(layer, h, half):
                v.tensor_copy(idx[:, half, :, :], tsrc[:, :, bass.ds(h * HALF, HALF)].rearrange("p t g -> p g t"))\
                 .then_inc(s_idx[layer], 1)

            dve.wait_ge(s_tcopied, 3 * GCH)
            for half in range(2):
                stage_idx(0, half, half)
            dve.wait_ge(s_grow, 1)
            v.memset(aggT[:, 0, :], 0.0).then_inc(s_aggclear, 1)

            dve.wait_ge(s_grow, 1)
            LOr, HIr, NVf, INC, STA = grow(1, i32), grow(0), grow(2), grow(3), grow(4)
            tc.then(v.tensor_copy(LOr[:, 0:NG], pROW[0]))
            tc.then(v.tensor_copy(HIr[:, 0:NG], pROW[1]))
            tc.then(v.tensor_copy(NVf[:, 0:NG], pROW[2]))
            tc.then(v.tensor_tensor_scan(INC[:, 0:NG], NVf[:, 0:NG], NVf[:, 0:NG], 0.0, ALU.add, ALU.bypass))
            tc.then(v.tensor_tensor(STA[:, 0:NG], INC[:, 0:NG], NVf[:, 0:NG], ALU.subtract))
            for r, frm in ((0, STA), (1, INC)):
                tc.then(v.tensor_copy(wins[0:1, :, r], frm[:, 0:NG]))
            LO4 = LOr[:, 0:NG].rearrange("o (h g) -> o h g", g=HALF)
            for r in range(2):
                pair = regs[0:1, :, 1 + r]
                tc.then(v.tensor_scalar(pair, LO4[:, :, 2 * r + 1], PACK, None, ALU.logical_shift_left))
                tc.then(v.tensor_tensor(pair, pair, LO4[:, :, 2 * r], ALU.bitwise_or))
            A, B, R = grow(5), grow(6), grow(7, i32)
            FL = grow(2)[:, 0:NH]
            tc.then(v.memset(work[0:1, 5 * GCH * P:7 * GCH * P], -float(P)))
            tc.then(v.tensor_reduce(A[:, 0:NH], HIr[:, 0:NG].rearrange("o (h g) -> o h g", g=HALF),
                                    axis=AX.X, op=ALU.max))
            d = 1
            while d <= NH:
                tc.then(v.tensor_tensor(B[:, 0:NH + 1], A[:, 0:NH + 1], A[:, d:d + NH + 1], ALU.max))
                A, B, d = B, A, 2 * d
            tc.then(v.tensor_copy(R[:, 0:NH], A[:, 1:NH + 1]))
            tc.then(v.tensor_scalar(R[:, 0:NH], R[:, 0:NH], 7, None, ALU.arith_shift_right))
            tc.then(v.tensor_copy(A[:, 0:NH], R[:, 0:NH]))
            tc.then(v.tensor_scalar(A[:, 0:NH], A[:, 0:NH], -1.0, float(NB - 1), ALU.mult, ALU.add))
            tc.then(v.tensor_scalar(B[:, 0:NH], tnum[0:1, 0:NH], float(LEAD), None, ALU.add))
            tc.then(v.tensor_tensor(A[:, 0:NH], A[:, 0:NH], B[:, 0:NH], ALU.min))
            INC4, STA4 = (a[:, 0:NG].rearrange("o (h g) -> o h g", g=HALF) for a in (INC, STA))
            tc.then(v.tensor_tensor(FL, INC4[:, :, HALF - 1], STA4[:, :, 0], ALU.subtract))
            tc.then(v.tensor_scalar(FL, FL, 1.0, 65536.0, ALU.min, ALU.mult))
            tc.then(v.tensor_tensor(FL, FL, A[:, 0:NH], ALU.add))
            tc.then(v.scalar_tensor_tensor(out=FL[:, 1:NH], in0=A[:, 0:NH - 1], scalar=256.0, in1=FL[:, 1:NH],
                                           op0=ALU.mult, op1=ALU.add))
            tc.then(v.tensor_copy(regs[0:1, :, 0], FL))
            tc.then(v.memset(work[:, :], 0.0))
            tc.then(v.memset(pZ[:, 0:C], 0.0))
            tc.then(v.memset(pT[:, 0:C], 0.0))
            v.memset(bmv[:, :], 1.0).then_inc(s_regs, 1)
            for sm in (s_zb[0], s_zb[1], s_xn2, s_hb, s_elu[0], s_elu[1], s_var2, s_xTc, s_lg):
                dve.sem_inc(sm, 1)
            dve.sem_inc(s_o, 2)

            dve.wait_ge(s_const, NCONST)
            dve.wait_ge(s_tcopied, 3 * GCH)
            dve.wait_ge(s_tbl_clear, 3)
            dve.wait_ge(s_regs, 1)
            dve.wait_ge(s_aggclear, 2)

            def build_S(layer, g, half):
                dve.wait_ge(s_mm[layer], g + (SLOTS - 1))
                for t in range(T):
                    last = v.tensor_scalar(S[:, half, t, :], iota_w[:, :], tdst[:, t, bass.ds(g, 1)],
                                           twgt[:, t, bass.ds(g, 1)], ALU.is_equal, ALU.mult)
                last.then_inc(s_S[layer], 1)

            def overflow(layer, g, base):
                ws, we = overflow_windows(dve, g)
                with dve.If(ws < we):
                    with dve.Fori(ws, we) as w:
                        k = within(w - ws + 1, 1, KWIN)
                        v.tensor_scalar(cur[:, :], tdst[:, :, bass.ds(g, 1)].rearrange("p t g -> p (t g)"),
                                        woff[:, bass.ds(k, 1)], None, ALU.subtract).then_inc(s_ovc[layer], 1)
                        dve.wait_ge(s_ovc[layer], w + 1)
                        for t in range(T):
                            last = v.tensor_scalar(Sov[:, t, :], iota_w[:, :], cur[:, t:t + 1],
                                                   twgt[:, t, bass.ds(g, 1)], ALU.is_equal, ALU.mult)
                        last.then_inc(s_ovS[layer], 1)
                        dve.wait_ge(s_ovmm[layer], w + 1)
                        at = within(base + k * W, 0, N - 1)
                        far = aggT[:, :, bass.ds(at, W)]
                        v.tensor_tensor(far, far, pOV.rearrange("p (k n) -> p k n", k=KC), ALU.add)\
                         .then_inc(s_ovadd[layer], 1)
                        hold(dve, s_ovadd[layer], w + 1)

            def edges_half(layer, h, with_overflow):
                for u in range(HALF):
                    g = HALF * h + u
                    if u % 2 == 0:
                        pair = dve.value_load(regs[0:1, bass.ds(h, 1), 1 + u // 2], min_val=0,
                                              max_val=(1 << 2 * PACK) - 1)
                        bases = [nc.s_assert_within(one, 0, N - 1, skip_runtime_bounds_check_because=
                                                    "a dst is below the number of nodes")
                                 for one in (pair & ((1 << PACK) - 1), pair >> PACK)]
                    hold(dve, s_add[layer], g + 2)
                    if with_overflow:
                        overflow(layer, g, bases[u % 2])
                    dve.wait_ge(s_mm[layer], g + 1 + SLOTS)
                    to = aggT[:, :, bass.ds(bases[u % 2], W)]
                    v.tensor_tensor(to, to, pA[:, u % 2, 0:KC * W].rearrange("p (k n) -> p k n", k=KC), ALU.add)\
                     .then_inc(s_add[layer], 1)
                    build_S(layer, g + 2, u % 2)

            def z_biased(layer, j):
                dve.wait_ge(s_z[layer], j + 1)
                dve.wait_ge(s_zexp[layer], j + 1)
                dve.wait_ge(s_elu[layer], j + 1)
                v.tensor_tensor(zb[:, :], pZ[:, 0:C], brow[:, layer * C:(layer + 1) * C], ALU.add)\
                 .then_inc(s_zb[layer], 1)

            def elu(layer, j, to):
                dve.wait_ge(s_zexp[layer], j + 2)
                v.tensor_scalar(zexp[:, :], zexp[:, :], -1.0, None, ALU.add).then_inc(s_eln[layer], 1)
                if layer == 0:
                    dve.wait_ge(s_free[0], j + 1)
                dve.wait_ge(s_eln[layer], j + 1)
                return v.scalar_tensor_tensor(out=to, in0=zb[:, :], scalar=0.0, in1=zexp[:, :],
                                              op0=ALU.max, op1=ALU.add)

            def tick1(j):
                z_biased(0, j)
                elu(0, j, hout).then_inc(s_elu[0], 1)
                if flows(0, j):
                    dve.wait_ge(s_blkclear, j + 1)

            bc = Steps(dve, s_tick)

            def tick2(j):
                bc.base, bc.n = 3 * j, 0
                if flows(1, j):
                    z_biased(1, j)
                if flows(3, j):
                    dve.wait_ge(s_xT, j + 1)
                    dve.wait_ge(s_hT, j + 1)
                    v.tensor_copy(xnT, pT[:, 0:C].rearrange("p (k n) -> p k n", k=KC)).then_inc(s_xTc, 1)
                if flows(4, j):
                    dve.wait_ge(s_hT, j + 1)
                    dve.wait_ge(s_gelu, j + 1)
                    v.tensor_tensor(hid, pB[:, :].rearrange("p (k n) -> p k n", k=KH),
                                    b1col[:, :].unsqueeze(2).to_broadcast([P, KH, P]), ALU.add).then_inc(s_hb, 1)
                if flows(1, j):
                    bc.then(elu(1, j, zb[:, :]))
                if flows(2, j):
                    dve.wait_ge(s_std2, j + 2)
                    bc.then(v.reciprocal(bstd[:, 1:2], bstd[:, 0:1]))
                    dve.wait_ge(s_xT, j + 1)
                    v.tensor_scalar(xn2, x1, bmv[:, 0:1], bstd[:, 1:2], ALU.subtract, ALU.mult).then_inc(s_xn2, 1)
                if flows(1, j):
                    dve.wait_ge(s_xb, 16 * (j + 1))
                    dve.wait_ge(s_free[1], j + 1)
                    dve.wait_ge(s_xn2, j + 2)
                    v.tensor_tensor(x1, zb[:, :], xb, ALU.add).then_inc(s_elu[1], 1)
                    dve.wait_ge(s_elu[1], j + 2)
                    bc.then(v.bn_stats(bstat[:, :], x1), own=True)
                    v.bn_aggr(bmv[:, :], bstat[:, :]).then_inc(s_var2, 1)
                dve.wait_ge(s_payc, j + 2)
                hold(dve, s_log, j + 2)
                v.tensor_reduce(lgpart[:, 0, :], pF[:, :, :, P:PG].rearrange("p b c e -> p e b c"),
                                axis=AX.XY, op=ALU.add)
                v.tensor_tensor(lgpart[:, 1, :], pLG, brow[:, 2 * C:2 * C + NX], ALU.add).then_inc(s_lgp, 1)
                dve.wait_ge(s_lgp, j + 1)
                v.tensor_tensor(LG[:, bass.ds(j * -1 + (NB - 1 + DEPTH), 1), :].rearrange("p b e -> p (b e)"), lgpart[:, 0, :],
                                lgpart[:, 1, :], ALU.add).then_inc(s_lg, 1)

            for layer in range(2):
                if layer:
                    dve.wait_ge(s_blkclear, NB)
                    dve.wait_ge(s_w, 8 * 16)
                    for s in range(SLOTS):
                        dve.wait_ge(s_gath[0][s], 16 * T * ITERS)
                    for half in range(2):
                        stage_idx(layer, half, half)
                dve.sem_inc(s_add[layer], 2)
                for half in range(2):
                    build_S(layer, half, half)
                with dve.Fori(0, ITERS) as i:
                    for half in range(2):
                        h = 2 * i + half
                        ovf, start, end = half_flags(dve, h)
                        with dve.If(ovf > 0):
                            edges_half(layer, h, True)
                        with dve.Else():
                            edges_half(layer, h, False)
                        stage_idx(layer, h + 2, half)
                        ticks(dve, start, end, (tick1, tick2)[layer])
                if layer == 0:
                    tick1(NB)
            for j in range(NB, NB + DEPTH):
                tick2(j)

            gc = Steps(dve, s_gate)
            dve.wait_ge(s_lg, NB + DEPTH + 1)
            dve.wait_ge(s_mm[1], NG + SLOTS)
            lg = LG[:, 0:NB, :]
            DL, EX, SC, OH, CNT, INC, PL = (gate(n) for n in range(7))
            MX, EM, SM, RS, GATE, SMX, VAL, AT, FARV, PLACE, TIL, LAN, NUM = (per_node(n) for n in range(13))
            PLi, TLi = (per_node(n).bitcast(i32) for n in (13, 14))

            def wide(a):
                return a.unsqueeze(2).to_broadcast([P, NB, NX])

            def across(a):
                return a.unsqueeze(1).to_broadcast([P, NB, NX])

            gc.then(v.tensor_reduce(MX, lg, axis=AX.X, op=ALU.max))
            v.tensor_tensor(DL, lg, wide(MX), ALU.subtract).then_inc(s_dlog, 1)
            gc.then(v.tensor_scalar(VAL, node[:, :], float(N), None, ALU.is_lt))
            gc.then(v.tensor_scalar(FARV, VAL, -FAR, FAR, ALU.mult, ALU.add))
            dve.wait_ge(s_gexp, 1)
            gc.then(v.tensor_reduce(EM, EX, axis=AX.X, op=ALU.max))
            gc.then(v.tensor_tensor(SC, EX, wide(EM), ALU.is_equal))
            gc.then(v.tensor_tensor(SC, SC, across(prefer[:, :]), ALU.mult))
            gc.then(v.tensor_reduce(SMX, SC, axis=AX.X, op=ALU.max))
            gc.then(v.tensor_tensor(SC, SC, wide(SMX), ALU.is_equal))
            v.tensor_tensor(OH, SC, wide(VAL), ALU.mult).then_inc(s_oh, 1)
            gc.then(v.tensor_reduce(SM, EX, axis=AX.X, op=ALU.add))
            gc.then(v.reciprocal(RS, SM))
            gc.then(v.tensor_tensor(GATE, EM, RS, ALU.mult))
            dve.wait_ge(s_rank, 1)
            HB = NB // 2
            for n in range(2):
                gc.then(v.tensor_copy(CNT[:, n * HB:(n + 1) * HB, :],
                                      pC[:, n * 512:n * 512 + HB * NX].rearrange("p (b e) -> p b e", e=NX)))
            for e in range(NX):
                last = v.tensor_tensor_scan(INC[:, :, e], CNT[:, :, e], CNT[:, :, e], 0.0, ALU.add, ALU.bypass)
            gc.then(last)
            gc.then(v.tensor_tensor(PL, INC, CNT, ALU.subtract))
            n_e, tiles, ends, starts, first = (zexp[:, 8 * n:8 * n + NX] for n in range(5))
            ti, tj = (zexp[:, 8 * n:8 * n + NX].bitcast(i32) for n in (5, 6))
            assert NX == 8
            gc.then(v.tensor_scalar(n_e, INC[:, NB - 1, :], float(P - 1), None, ALU.add))
            gc.then(v.tensor_copy(ti, n_e))
            gc.then(v.tensor_scalar(tj, ti, 7, None, ALU.arith_shift_right))
            gc.then(v.tensor_copy(tiles, tj))
            gc.then(v.tensor_tensor_scan(ends, tiles, tiles, 0.0, ALU.add, ALU.bypass))
            gc.then(v.tensor_tensor(starts, ends, tiles, ALU.subtract))
            gc.then(v.tensor_scalar(first, starts, float(P), None, ALU.mult))
            gc.then(v.tensor_tensor(PL, PL, across(first), ALU.add))
            for n in range(2):
                half = PL[:, n * HB:(n + 1) * HB, :]
                gc.then(v.tensor_tensor(half, half, pB[:, n * 512:n * 512 + HB * NX]
                                        .rearrange("p (b e) -> p b e", e=NX), ALU.add))
            gc.then(v.tensor_tensor(PL, PL, OH, ALU.mult))
            gc.then(v.tensor_reduce(AT, PL, axis=AX.X, op=ALU.add))
            gc.then(v.tensor_tensor(PLACE, AT, FARV, ALU.add))
            gc.then(v.tensor_copy(PLi, PLACE))
            gc.then(v.tensor_scalar(TLi, PLi, 7, None, ALU.arith_shift_right))
            gc.then(v.tensor_copy(TIL, TLi))
            gc.then(v.scalar_tensor_tensor(out=LAN, in0=TIL, scalar=-float(P), in1=PLACE,
                                           op0=ALU.mult, op1=ALU.add))
            gc.then(v.tensor_scalar(NUM, node[:, :], -float(N), None, ALU.add))

            for i in runs(dve, NB // (2 * LB)):
                for n in range(2):
                    c = 2 * i + n
                    need(dve, s_lmm, c - 1)
                    need(dve, s_tgate, c - 1)

                    def blocks(a, width):
                        return a[:, bass.ds(c * LB, LB)].unsqueeze(2).to_broadcast([P, LB, width])

                    v.tensor_tensor(in_tile[:, n, :, :], tnum[:, :].unsqueeze(1).to_broadcast([P, LB, NT]),
                                    blocks(TIL, NT), ALU.is_equal).then_inc(s_in, 1)
                    v.tensor_tensor(lane_is[:, n, :, :], iota_p[:, :].unsqueeze(1).to_broadcast([P, LB, P]),
                                    blocks(LAN, P), ALU.is_equal)
                    hold(dve, s_in, c + 1)
                    v.tensor_tensor(tile_is[:, n, :, 0, :], in_tile[:, n, :, :], blocks(NUM, NT), ALU.mult)\
                     .then_inc(s_tile, 1)

            et = Steps(dve, s_et)
            starts = starts[0:1, :]
            ex, tmp = zneg[0:1, 0:NT], zneg[0:1, NT:2 * NT]
            et.then(v.memset(ex, 0.0))
            for e in range(1, NX):
                et.then(v.tensor_scalar(tmp, tnum[0:1, :], starts[:, e:e + 1], None, ALU.is_ge))
                et.then(v.tensor_tensor(ex, ex, tmp, ALU.add))
            v.tensor_scalar(etab[0:1, :], ex, float(C), None, ALU.mult).then_inc(s_etr, 1)

            dve.wait_ge(s_lmm, NB // LB)
            et.then(v.tensor_scalar(lists[:, 0, :], pL[:, 0:NT], float(N), None, ALU.add))
            et.then(v.tensor_copy(lists[:, 1, :], pL[:, NT:2 * NT]))

            def stage_ids(t, r):
                v.tensor_copy(ids[:, r:r + 1], lists[:, 0, bass.ds(t, 1)]).then_inc(s_ids, 1)

            for q in range(QB):
                stage_ids(q, q)

            dve.wait_ge(s_wd, 16 * (KH + 1))
            dve.wait_ge(s_etr, 1)

            def copy_half(t, b2):
                dve.wait_ge(s_eT, t + 1)
                v.tensor_copy(HTx[:, b2, KH // 2:KH, :],
                              (pB, pC)[b2][:, 512:1024].rearrange("p (k n) -> p k n", k=KH // 2)).then_inc(s_eTd, 1)

            def output(t, q):
                ec = dve.value_load(etab[0:1, bass.ds(t, 1)], min_val=0, max_val=(NX - 1) * C)
                dve.wait_ge(s_y, t + 3)
                v.tensor_tensor(obuf[:, q, :], pA[:, q % 2, 0:C], bd[:, bass.ds(ec, C)], ALU.add).then_inc(s_yb, 1)
                dve.wait_ge(s_yb, t + 1)
                v.scalar_tensor_tensor(out=obuf[:, q, :], in0=obuf[:, q, :], scalar=lists[:, 1, bass.ds(t, 1)],
                                       in1=payx[:, q, HID:PAY], op0=ALU.mult, op1=ALU.add).then_inc(s_o, 1)

            copy_half(0, 0)
            for i in runs(dve, NT // RING):
                for r in range(RING):
                    t, q = RING * i + r, r % QB
                    copy_half(t + 1, (r + 1) % 2)
                    need(dve, s_out[q], 16 * (2 * i + r // QB))
                    output(t, q)
                    if not isinstance(t, int) or t + QB < NT:
                        stage_ids(t + QB, (r + QB) % RING)
            dve.wait_ge(s_out[0], 16 * (NT // QB))
            output(NT - 1, 0)

        @block.tensor
        def _(pe):
            mm = nc.tensor.matmul
            for layer in range(2):
                pe.sem_inc(s_mm[layer], SLOTS)
            pe.wait_ge(s_const, 3)
            pe.wait_ge(s_gvec, 1)
            for c in range(GCH):
                cnt = P if c < GCH - 1 else TAILG
                at = NG - c * P - cnt
                for to, vector in zip(pROW, (gvec(0), gvec(1), gvec(3))):
                    last = mm(to[:, at:at + cnt], vector[0:cnt, c:c + 1], flip[0:cnt, P - cnt:P],
                              start=True, stop=True)
            last.then_inc(s_grow, 1)
            pe.wait_ge(s_float, 2 + GCH)
            pe.wait_ge(s_rows, 9 * 16)
            n = 0
            for rowtable in (rrel, rsrc, rwgt):
                for c in range(GCH):
                    cnt = P if c < GCH - 1 else TAILG
                    need(pe, s_tcopied, n - 1)
                    for t in range(T):
                        at = (n % 2) * 512 + t * P
                        last = mm(pB[:, at:at + cnt], rowtable[0:cnt, c, t * P:(t + 1) * P],
                                  flip[0:cnt, P - cnt:P], start=True, stop=True)
                    last.then_inc(s_tT, 1)
                    n += 1
            pe.wait_ge(s_tcopied, 3 * GCH)
            pe.wait_ge(s_regs, 1)
            pe.wait_ge(s_const, NCONST)

            for sm in (s_xT, s_hT, s_z[0], s_z[1], s_log, s_hback):
                pe.sem_inc(sm, 1)
            pe.sem_inc(s_y, 2)

            def products(slot, Sx, to, semaphore):
                for k in range(KC):
                    for t in range(T):
                        last = mm(to[:, k * W:(k + 1) * W], rows[:, slot, t, k * P:(k + 1) * P], Sx[:, t, :],
                                  start=(t == 0), stop=(t == T - 1))
                last.then_inc(semaphore, 1)

            def z_part(layer, j):
                wg = (wg1, wg2)[layer]
                pe.wait_ge(s_stage[layer], j + 2)
                pe.wait_ge(s_zb[layer], j + 2)
                for k in range(KC):
                    last = mm(pZ[:, 0:C], stage[:, k, :], wg[:, k, :], start=(k == 0), stop=(k == KC - 1))
                last.then_inc(s_z[layer], 1)

            def tick1(j):
                z_part(0, j)

            def tick2(j):
                if flows(4, j - 1):
                    pe.wait_ge(s_gelu, j + 1)
                pe.wait_ge(s_payc, j + 1)
                for m in range(FUSED):
                    mm(pF[:, m // PERB, m % PERB, :], HT[:, m, :], identg[:, m, :], start=True, stop=True)
                if flows(3, j):
                    pe.wait_ge(s_xTc, j + 2)
                for m in range(FUSED, KH):
                    at = C + (m - FUSED) * P
                    last = nc.tensor.transpose(pT[:, at:at + P], HT[:, m, :], ident[:, :])
                last.then_inc(s_hback, 1)
                for m in range(FUSED, KH):
                    last = mm(pLG, HT[:, m, :], identg[:, m, P:PG], start=(m == FUSED), stop=(m == KH - 1))
                last.then_inc(s_log, 1)
                if flows(3, j):
                    pe.wait_ge(s_hb, j + 2)
                    for m in range(KH):
                        for k in range(KC):
                            last = mm(pB[:, m * P:(m + 1) * P], w1[:, k, m * P:(m + 1) * P], xnT[:, k, :],
                                      start=(k == 0), stop=(k == KC - 1))
                    last.then_inc(s_hT, 1)
                if flows(0, j):
                    z_part(1, j)
                if flows(2, j):
                    pe.wait_ge(s_xn2, j + 2)
                    pe.wait_ge(s_payc, j + 2)
                    for k in range(KC):
                        last = nc.tensor.transpose(pT[:, k * P:(k + 1) * P], xn2[:, k * P:(k + 1) * P], ident[:, :])
                    last.then_inc(s_xT, 1)
                pe.wait_ge(s_lg, j + 2)

            def edges_half(layer, i, h, half, with_overflow):
                for u in range(HALF):
                    s, g = half * HALF + u, HALF * h + u
                    pe.wait_ge(s_gath[layer][s], 16 * T * (i + 1))
                    if with_overflow:
                        ws, we = overflow_windows(pe, g)
                        with pe.If(ws < we):
                            with pe.Fori(ws, we) as w:
                                pe.wait_ge(s_ovS[layer], w + 1)
                                products(s, Sov, pOV, s_ovmm[layer])
                    pe.wait_ge(s_S[layer], g + 1)
                    pe.wait_ge(s_add[layer], g + 1)
                    products(s, S[:, s % 2, :, :], pA[:, s % 2, :], s_mm[layer])

            pe.wait_ge(s_w, 8 * 16)
            for layer in range(2):
                with pe.Fori(0, ITERS) as i:
                    for half in range(2):
                        h = 2 * i + half
                        ovf, start, end = half_flags(pe, h)
                        with pe.If(ovf > 0):
                            edges_half(layer, i, h, half, True)
                        with pe.Else():
                            edges_half(layer, i, h, half, False)
                        ticks(pe, start, end, (tick1, tick2)[layer])
            for j in range(NB, NB + DEPTH):
                tick2(j)

            pe.wait_ge(s_oh, 1)
            pe.wait_ge(s_payc, NB + DEPTH + 1)
            pe.wait_ge(s_hb, NB + 5)
            HB = NB // 2
            for to, what in ((pB, before), (pC, ones)):
                for n in range(2):
                    last = mm(to[:, n * 512:n * 512 + HB * NX], what[:, :],
                              gate(3)[:, n * HB:(n + 1) * HB, :].rearrange("p b e -> p (b e)"), start=True, stop=True)
            last.then_inc(s_rank, 1)

            pe.wait_ge(s_xTc, NB + 3)
            for i in runs(pe, NB // (2 * LB)):
                for n in range(2):
                    pe.wait_ge(s_tile, 2 * i + n + 1)
                    pe.wait_ge(s_tgate, 2 * i + n + 1)
                    for k in range(LB):
                        outer = isinstance(i, int)
                        last = mm(pL, lane_is[:, n, k, :], tile_is[:, n, k, :, :].rearrange("p v n -> p (v n)"),
                                  start=(outer and i == 0 and n == 0 and k == 0),
                                  stop=(outer and i > 0 and n == 1 and k == LB - 1))
                    last.then_inc(s_lmm, 1)

            pe.wait_ge(s_wd, 16 * (KH + 1))
            pe.wait_ge(s_etr, 1)

            def transpose_tile(i, q):
                pe.wait_ge(s_pg[q], 16 * (i + 1))
                for m in range(KH):
                    last = nc.tensor.transpose((pB, pC)[q % 2][:, m * P:(m + 1) * P],
                                               payx[:, q, m * P:(m + 1) * P], ident[:, :])
                last.then_inc(s_eT, 1)

            def expert(t, q):
                ec = pe.value_load(etab[0:1, bass.ds(t, 1)], min_val=0, max_val=(NX - 1) * C)
                pe.wait_ge(s_o, t + 1)
                pe.wait_ge(s_eTa, t + 1)
                pe.wait_ge(s_eTd, t + 1)
                for m in range(KH):
                    last = mm(pA[:, q % 2, 0:C], HTx[:, q % 2, m, :], wdk[:, m, bass.ds(ec, C)],
                              start=(m == 0), stop=(m == KH - 1))
                last.then_inc(s_y, 1)

            transpose_tile(0, 0)
            with pe.Fori(0, NT // QB) as i:
                for q in range(QB):
                    transpose_tile(i + (q + 1) // QB, (q + 1) % QB)
                    expert(QB * i + q, q)
            expert(NT - 1, 0)


_INS = ['x', 'src', 'dst', 'edge_weight', 'L0_gnn_W1', 'L0_gnn_b1', 'L0_gnn_W2', 'L0_gnn_b2',
        'L0_ffn_W1', 'L0_ffn_b1', 'L0_ffn_Wg', 'L0_ffn_bg', 'L0_ffn_Wd', 'L0_ffn_bd']


def kernel(**inputs):
    import numpy as _np
    import concourse.bacc as _bacc
    from concourse import mybir as _mybir
    from concourse.bass_utils import run_bass_kernel_spmd as _run

    nc = _bacc.Bacc("TRN2", target_bir_lowering=False, num_devices=1)
    arrays, args = {}, []
    for name in _INS:
        a = _np.ascontiguousarray(inputs[name])
        arrays[f"in_{name}_dram"] = a
        args.append(nc.dram_tensor(f"in_{name}_dram", a.shape, _mybir.dt.from_np(a.dtype), kind="ExternalInput").ap())
    args.append(nc.dram_tensor("out_0_dram", inputs['x'].shape, _mybir.dt.float32, kind="ExternalOutput").ap())
    bass_gnn_then_routed_ffn(nc, *args)
    nc.compile()
    r = _run(nc, [arrays], core_ids=[0])
    return r.results[0]["out_0_dram"]
```
